# Optimizing a Trainium2 kernel written in Bass

```python
import numpy as np
import jax
import jax.numpy as jnp

def _softmax(x, axis=-1):
    return jax.nn.softmax(x, axis=axis)

def _gelu(x):
    return jax.nn.gelu(x, approximate=True)

def _silu(x):
    return jax.nn.silu(x)

def _sigmoid(x):
    return jax.nn.sigmoid(x)

def _layernorm(x, axis=-1, eps=1e-05):
    m = jnp.mean(x, axis=axis, keepdims=True)
    v = jnp.var(x, axis=axis, keepdims=True)
    return (x - m) / jnp.sqrt(v + eps)

def _scatter_add(tgt, idx, src, axis=0):
    return tgt.at[idx].add(src)

def _segment_sum(src, seg, n):
    return jax.ops.segment_sum(src, seg, n)
kernel_name = 'mk_xattn_ffn_d1_seqx_r2_41a40b'

def setup_inputs(seed: int=0):
    np.random.seed(seed)
    _w = jnp.asarray

    def _rec_inputs():
        import jax
        import jax.numpy as jnp
        _rk = jax.random.key(seed)
        x = 7.22e-05 + 1 * jax.random.normal(jax.random.fold_in(_rk, 1), (2, 2048, 512), jnp.float32)
        _lenS = 2048 - jax.random.randint(jax.random.fold_in(_rk, 7), (2,), 0, max(1, 2048 // 4) + 1, jnp.int32)
        _lenS2 = 77 - jax.random.randint(jax.random.fold_in(_rk, 8), (2,), 0, max(1, 77 // 4) + 1, jnp.int32)
        _ctx_1024P = jax.random.normal(jax.random.fold_in(_rk, 11), (2, 16, 512), jnp.float32)
        _ctx_1024c = jax.random.dirichlet(jax.random.fold_in(_rk, 511), 0.3 * jnp.ones((16,), jnp.float32), (2, 77))
        _ctx_1024t = jnp.einsum('bsk,bkd->bsd', _ctx_1024c, _ctx_1024P)
        _ctx_1024t = _ctx_1024t * jax.lax.rsqrt(jnp.mean(jnp.square(_ctx_1024t)) + 1e-12) * 0.953939
        ctx_1024 = 4.13588e-05 + 0.999923 * (_ctx_1024t + 0.3 * jax.random.normal(jax.random.fold_in(_rk, 611), (2, 77, 512), jnp.float32))
        _ctxb_2048x32P = jax.random.normal(jax.random.fold_in(_rk, 12), (2, 16, 32), jnp.float32)
        _ctxb_2048x32c = jax.random.dirichlet(jax.random.fold_in(_rk, 512), 0.3 * jnp.ones((16,), jnp.float32), (2, 77))
        _ctxb_2048x32t = jnp.einsum('bsk,bkd->bsd', _ctxb_2048x32c, _ctxb_2048x32P)
        _ctxb_2048x32t = _ctxb_2048x32t * jax.lax.rsqrt(jnp.mean(jnp.square(_ctxb_2048x32t)) + 1e-12) * 0.953939
        ctxb_2048x32 = 0.000843197 + 0.998132 * (_ctxb_2048x32t + 0.3 * jax.random.normal(jax.random.fold_in(_rk, 612), (2, 77, 32), jnp.float32))
        return (x, ctx_1024, ctxb_2048x32)
    x, ctx_1024, ctxb_2048x32 = _rec_inputs()

    def _L0_xattn_setup():
        import jax, jax.numpy as jnp
        import numpy as np
        B, L, D, H, NF = (4, 1024, 512, 16, 32)
        THRESHOLD = 0.1
        key = jax.random.key(seed)
        ks = jax.random.split(key, 12)
        s = 1.0 / np.sqrt(D)
        return {'q_x': jax.random.normal(ks[0], (B, L, D), jnp.float32), 'k_x': jax.random.normal(ks[1], (B, L, D), jnp.float32), 'v_x': jax.random.normal(ks[2], (B, L, D), jnp.float32), 'energy_coeffs': jax.random.normal(ks[3], (B, L, NF), jnp.float32), 'Wq': jax.random.normal(ks[4], (D, D), jnp.float32) * s, 'bq': jnp.zeros((D,), jnp.float32), 'Wk': jax.random.normal(ks[5], (D, D), jnp.float32) * s, 'bk': jnp.zeros((D,), jnp.float32), 'Wv': jax.random.normal(ks[6], (D, D), jnp.float32) * s, 'bv': jnp.zeros((D,), jnp.float32), 'Wo': jax.random.normal(ks[7], (D, D), jnp.float32) * s, 'bo': jnp.zeros((D,), jnp.float32)}
    _L0_xattn_all = _L0_xattn_setup()
    _L0_xattn_in = {k: v for k, v in _L0_xattn_all.items() if k in ('Wq', 'bq', 'Wk', 'bk', 'Wv', 'bv', 'Wo', 'bo')}
    del _L0_xattn_all

    def _L0_ffn_setup():
        import jax, jax.numpy as jnp
        import numpy as np
        E = 8
        K = 2
        CF = 1.25
        key = jax.random.key(seed)
        kx, kr, kg, ku, kd = jax.random.split(key, 5)
        D, F = (512, 2048)
        x = jax.random.normal(kx, (4, 1024, D), dtype=jnp.float32)
        router_w = 0.02 * jax.random.normal(kr, (E, D), dtype=jnp.float32)
        wg = jax.random.normal(kg, (E, D, F), dtype=jnp.float32) / np.sqrt(D)
        wu = jax.random.normal(ku, (E, D, F), dtype=jnp.float32) / np.sqrt(D)
        wd = jax.random.normal(kd, (E, F, D), dtype=jnp.float32) / np.sqrt(F)
        return {'x': x, 'router_w': router_w, 'wg': wg, 'wu': wu, 'wd': wd}
    _L0_ffn_all = _L0_ffn_setup()
    _L0_ffn_in = {k: v for k, v in _L0_ffn_all.items() if k in ('router_w', 'wg', 'wu', 'wd')}
    del _L0_ffn_all
    return {'x': x, 'ctx_1024': ctx_1024, 'ctxb_2048x32': ctxb_2048x32, 'L0_xattn_Wq': _L0_xattn_in['Wq'], 'L0_xattn_bq': _L0_xattn_in['bq'], 'L0_xattn_Wk': _L0_xattn_in['Wk'], 'L0_xattn_bk': _L0_xattn_in['bk'], 'L0_xattn_Wv': _L0_xattn_in['Wv'], 'L0_xattn_bv': _L0_xattn_in['bv'], 'L0_xattn_Wo': _L0_xattn_in['Wo'], 'L0_xattn_bo': _L0_xattn_in['bo'], 'L0_ffn_router_w': _L0_ffn_in['router_w'], 'L0_ffn_wg': _L0_ffn_in['wg'], 'L0_ffn_wu': _L0_ffn_in['wu'], 'L0_ffn_wd': _L0_ffn_in['wd']}

def reference(x, ctx_1024, ctxb_2048x32, L0_xattn_Wq, L0_xattn_bq, L0_xattn_Wk, L0_xattn_bk, L0_xattn_Wv, L0_xattn_bv, L0_xattn_Wo, L0_xattn_bo, L0_ffn_router_w, L0_ffn_wg, L0_ffn_wu, L0_ffn_wd):
    import jax
    import jax.numpy as jnp

    def _L0_xattn_ref(q_x, k_x, v_x, energy_coeffs, Wq, bq, Wk, bk, Wv, bv, Wo, bo):
        import jax, jax.numpy as jnp
        import numpy as np
        B, L, D, H, NF = (4, 1024, 512, 16, 32)
        THRESHOLD = 0.1
        Bq, Lq, Dm = q_x.shape
        Dh = Dm // H
        Q = (q_x @ Wq + bq).reshape(Bq, Lq, H, Dh).transpose(0, 2, 1, 3)
        K = (k_x @ Wk + bk).reshape(Bq, -1, H, Dh).transpose(0, 2, 1, 3)
        V = (v_x @ Wv + bv).reshape(Bq, -1, H, Dh).transpose(0, 2, 1, 3)
        scores = jnp.einsum('bhqd,bhkd->bhqk', Q, K) / jnp.sqrt(jnp.float32(Dh))
        energy = jnp.abs(energy_coeffs).mean(axis=-1)
        energy = energy / (energy.max(axis=-1, keepdims=True) + 1e-08)
        gate = (energy > THRESHOLD).astype(scores.dtype) * 0.9 + 0.1
        scores = scores * gate[:, None, None, :]
        attn = jax.nn.softmax(scores, axis=-1)
        attn = jnp.nan_to_num(attn, nan=0.0)
        out = jnp.einsum('bhqk,bhkd->bhqd', attn, V)
        out = out.transpose(0, 2, 1, 3).reshape(Bq, Lq, Dm)
        return out @ Wo + bo

    def _L0_ffn_ref(x, router_w, wg, wu, wd):
        import jax, jax.numpy as jnp
        import numpy as np
        E = 8
        K = 2
        CF = 1.25
        B, L, D = x.shape
        xf = x.reshape(-1, D)
        N = xf.shape[0]
        capacity = max(1, int(CF * N / E))
        logits = xf @ router_w.T
        probs = jax.nn.softmax(logits, axis=-1)
        topw, topi = jax.lax.top_k(probs, K)
        topw = topw / (topw.sum(-1, keepdims=True) + 1e-06)
        fe = topi.reshape(-1)
        fw = topw.reshape(-1)
        ft = jnp.repeat(jnp.arange(N), K)
        order = jnp.lexsort((-fw, fe))
        se, sw, st = (fe[order], fw[order], ft[order])
        counts = jax.ops.segment_sum(jnp.ones_like(se), se, num_segments=E)
        starts = jnp.cumsum(counts) - counts
        rank = jnp.arange(N * K) - starts[se]
        keep = rank < capacity
        pos = jnp.where(keep, rank, capacity)
        disp = jnp.zeros((E, capacity + 1, D), x.dtype).at[se, pos].set(xf[st])
        disp = disp[:, :capacity]
        g = jnp.einsum('ecd,edf->ecf', disp, wg)
        u = jnp.einsum('ecd,edf->ecf', disp, wu)
        eo = jnp.einsum('ecf,efd->ecd', jax.nn.silu(g) * u, wd)
        gathered = eo[se, jnp.minimum(pos, capacity - 1)]
        contrib = gathered * (sw * keep.astype(x.dtype))[:, None]
        out = jnp.zeros_like(xf).at[st].add(contrib)
        return out.reshape(B, L, D)
    x = x + _L0_xattn_ref(_layernorm(x, axis=-1), ctx_1024, ctx_1024, ctxb_2048x32, L0_xattn_Wq, L0_xattn_bq, L0_xattn_Wk, L0_xattn_bk, L0_xattn_Wv, L0_xattn_bv, L0_xattn_Wo, L0_xattn_bo)
    x = x + _L0_ffn_ref(_layernorm(x, axis=-1), L0_ffn_router_w, L0_ffn_wg, L0_ffn_wu, L0_ffn_wd)
    return x

_drawn_inputs = setup_inputs


def setup_inputs(seed=0):
    import zlib

    import numpy as np

    out = dict(_drawn_inputs(seed))
    spreads = {'L0_xattn_bq': (0.0, 0.1),
     'L0_xattn_bk': (0.0, 0.1),
     'L0_xattn_bv': (0.0, 0.1),
     'L0_xattn_bo': (0.0, 0.1)}
    factors = {}
    for name, (base, spread) in spreads.items():
        noise = np.random.default_rng([zlib.crc32(name.encode()), seed]).standard_normal(out[name].shape)
        drawn = base * np.exp(spread * noise) if base else spread * noise
        out[name] = jnp.asarray(drawn.astype(out[name].dtype))
    for name, factor in factors.items():
        out[name] = (out[name] * factor).astype(out[name].dtype)
    return out
```

```python
import concourse.bass as bass
from concourse import mybir
from contextlib import ExitStack

f32 = mybir.dt.float32
f32r = mybir.dt.float32r
bf16 = mybir.dt.bfloat16
i32 = mybir.dt.int32
ALU = mybir.AluOpType
ACT = mybir.ActivationFunctionType
AX = mybir.AxisListType

P = 128
B, L, D = 2, 2048, 512
N = B * L
TILES = N // P
H, DH = 16, 32
S = 77
NF = 32
KC = D // P
HG = P // DH
GS = HG * S
CH = 103
CHUNK0 = [0, CH, GS - CH]
E, F, TOPK = 8, 2048, 2
CAP = max(1, int(1.25 * N / E))
CT = CAP // P
NA = 256
NB = CAP - NA
FC = F // P
SEG = 16
NV = 6
ES = 1e-5
BITS = 30
PAIRS_OF_BITS = BITS // 2
SEARCH = 5
HOT = TILES // 4
TILE_BITS = P.bit_length() - 1
THRESHOLD = 0.1
RN = 96
PARTS = ((0, 0), (0, 1), (1, 0))


class Tile:

    def __init__(self, k, c):
        self.k, self.c = k, c

    def count(self, per, extra):
        return self.k * (4 * per) + (self.c * per + extra)

    def halves(self, per, extra):
        return self.k * (2 * per) + ((self.c // 2) * per + extra)

    def quarters(self, per, extra):
        return self.k * per + ((self.c // 4) * per + extra)

    def back(self, n):
        return Tile(self.k, self.c - n)

    def exists(self):
        return not isinstance(self.k, int) or 0 <= self.c < TILES

    def batch(self):
        return self.c % 2

    def row(self):
        return self.k * 2 + self.c // 2


def after(eng, sem, n):
    if isinstance(n, int) and n <= 0:
        return
    eng.wait_ge(sem, n)


def after_apart(eng, sem, n, met, value):
    if isinstance(n, int):
        after(eng, sem, n)
        return
    n = eng.compute_val(n)
    eng.wait_ge(met, value)
    eng.wait_ge(sem, n)


FIRST, LOOP, LOOPS, LAST = -1, 4, 6, TILES + 3


def steps(eng, step):
    for c in range(FIRST, LOOP):
        step(Tile(0, c))
    with eng.Fori(0, LOOPS) as k:
        for c in range(LOOP, LOOP + 4):
            step(Tile(k, c))
    for c in range(LOOP + 4 * LOOPS, LAST):
        step(Tile(0, c))


def attention(nc, ctx, x, context, energy, Wq, bq, Wk, bk, Wv, bv, Wo, bo, router_w, out,
              xn2, vblocks, logits):

    def sb(name, shape, dt=f32):
        return ctx.enter_context(nc.sbuf_tensor(name, shape, dt))

    def sem(name):
        return ctx.enter_context(nc.semaphore(name))

    wq = sb("wq", [P, KC, D])
    wo = sb("wo", [P, KC, D])
    wo_hi = sb("wo_hi", [P, KC, D], f32r)
    wo_lo = sb("wo_lo", [P, KC, D], f32r)
    wk = sb("wk", [P, KC, D])
    wv = sb("wv", [P, KC, D])
    bq_sb = sb("bq_sb", [P, KC])
    bk_sb = sb("bk_sb", [P, KC])
    bv_sb = sb("bv_sb", [S, D])
    bo_sb = sb("bo_sb", [P, D])
    rw = sb("rw", [E, D])
    rwT = sb("rwT", [P, KC, RN])
    ctx_sb = sb("ctx_sb", [S, B, D])
    ctxT = sb("ctxT", [P, KC, B, S])
    en = sb("en", [S, B, NF])
    esum = sb("esum", [S, B])
    ewide = sb("ewide", [S, B, P])
    ek = sb("ek", [P, B, S])
    emax = sb("emax", [P, B, 1])
    gate = sb("gate", [P, B, S])
    kT = sb("kT", [P, B, KC, S])
    kblock = sb("kblock", [P, B, KC, GS])
    k_hi = sb("k_hi", [P, B, KC, GS], f32r)
    k_lo = sb("k_lo", [P, B, KC, GS], f32r)
    vsb = sb("vsb", [S, B, D])
    vblock = sb("vblock", [CH, B, KC, 3, P])
    ident = sb("ident", [P, P])
    minus_half = sb("minus_half", [P, 1])
    xs = sb("xs", [P, 4, D])
    xb = sb("xb", [P, 4, D])
    st1, mv1, ve1, rs1 = sb("st1", [P, 6]), sb("mv1", [P, 2, 2]), sb("ve1", [P, 2, 1]), sb("rs1", [P, 2, 1])
    st2, mv2, ve2, rs2 = sb("st2", [P, 6]), sb("mv2", [P, 2, 2]), sb("ve2", [P, 2, 1]), sb("rs2", [P, 2, 1])
    xh = sb("xh", [P, 2, D])
    xT = sb("xT", [P, 2, KC, P])
    qT = sb("qT", [P, KC, P])
    q_hi = sb("q_hi", [P, 2, KC, P], f32r)
    q_lo = sb("q_lo", [P, 2, KC, P], f32r)
    probs = sb("probs", [P, 2, H, S])
    smax = sb("smax", [P, H])
    ssum = sb("ssum", [P, H])
    srec = sb("srec", [P, H])
    sinv = sb("sinv", [P, H])
    pT = sb("pT", [CH, 2, KC, 3, P])
    zeros = pT[:].rearrange("p j m q n -> p (j m q n)")[0:S, 0:SEG * P]
    o_hi = sb("o_hi", [P, 2, KC, P], f32r)
    o_lo = sb("o_lo", [P, 2, KC, P], f32r)
    x2 = sb("x2", [P, 2, D])
    x2h = sb("x2h", [P, 2, D])
    x2T = sb("x2T", [P, KC, P])

    ps_s = ctx.enter_context(nc.psum_tensor("ps_s", [P, KC, 512], f32))
    bank = [ctx.enter_context(nc.psum_tensor(f"bank{i}", [P, 512], f32)) for i in range(4, 8)]
    b4, b5, b6, b7 = bank

    ld_ctx, ld_wk, ld_wv, ld_wq, ld_wo = sem("ld_ctx"), sem("ld_wk"), sem("ld_wv"), sem("ld_wq"), sem("ld_wo")
    ld_small, ld_en = sem("ld_small"), sem("ld_en")
    consts_made, ident_made = sem("consts_made"), sem("ident_made")
    ctx_turned, ctxT_made = sem("ctx_turned"), sem("ctxT_made")
    energy_turned = sem("energy_turned")
    kv_product, v_made, gate_step, kblock_made = sem("kv_product"), sem("v_made"), sem("gate_step"), sem("kblock_made")
    zero_stored, v_stored, vblock_loaded, vblock_ready = sem("zero_stored"), sem("v_stored"), sem("vblock_loaded"), sem("vblock_ready")
    x_loaded = [sem(f"x_loaded{i}") for i in range(4)]
    st1_done, mv1_done, ve1_done, rs1_done, xh_done, xb_done = (
        sem("st1_done"), sem("mv1_done"), sem("ve1_done"), sem("rs1_done"), sem("xh_done"), sem("xb_done"))
    xh_turned, xT_made, q_product, qT_made = sem("xh_turned"), sem("xT_made"), sem("q_product"), sem("qT_made")
    q_hi_made, q_lo_made, o_hi_made, o_lo_made = sem("q_hi_made"), sem("q_lo_made"), sem("o_hi_made"), sem("o_lo_made")
    k_hi_made, k_lo_made, wo_hi_made, wo_lo_made = sem("k_hi_made"), sem("k_lo_made"), sem("wo_hi_made"), sem("wo_lo_made")
    scores_done, max_done, shifted, exp_done = sem("scores_done"), sem("max_done"), sem("shifted"), sem("exp_done")
    sum_done, rec_done, inv_done, probs_done = sem("sum_done"), sem("rec_done"), sem("inv_done"), sem("probs_done")
    probs_turned, pT_made, av_product = sem("probs_turned"), sem("pT_made"), sem("av_product")
    o_product, x2_done, st2_done, mv2_done, ve2_done, rs2_done, x2h_done = (
        sem("o_product"), sem("x2_done"), sem("st2_done"), sem("mv2_done"), sem("ve2_done"), sem("rs2_done"), sem("x2h_done"))
    x2h_turned, x2T_made, logit_product, logits_copied = (
        sem("x2h_turned"), sem("x2T_made"), sem("logit_product"), sem("logits_copied"))
    x2_stored = [sem(f"x2_stored{i}") for i in range(2)]
    x2h_stored = [sem(f"x2h_stored{i}") for i in range(2)]

    x_v = x.rearrange("b (r p) d -> b r p d", p=P)
    out_v = out.rearrange("b (r p) d -> b r p d", p=P)
    xn2_v = xn2.rearrange("(b r p) d -> b r p d", b=B, p=P)
    SMALL = 16 * 5

    with nc.Block() as block:

        @block.sync
        def _(sp):
            def load_x(t):
                s = t.c % 4
                after(sp, xb_done, t.count(1, 1 - 4))
                sp.dma_start(xs[:, s, :], x_v[t.batch(), t.row()]).then_inc(x_loaded[s], 16)

            sp.dma_start(ctx_sb[:], context.rearrange("b s d -> s b d")).then_inc(ld_ctx, 16)
            sp.dma_start(wk[:], Wk.rearrange("(k p) n -> p k n", p=P)).then_inc(ld_wk, 16)
            load_x(Tile(0, 0))
            sp.dma_start(wv[:], Wv.rearrange("(k p) n -> p k n", p=P)).then_inc(ld_wv, 16)
            sp.dma_start(wq[:], Wq.rearrange("(k p) n -> p k n", p=P)).then_inc(ld_wq, 16)
            for c in range(1, 4):
                load_x(Tile(0, c))
            sp.dma_start(wo[:], Wo.rearrange("(k p) n -> p k n", p=P)).then_inc(ld_wo, 16)
            sp.wait_ge(consts_made, 4)
            for b in range(B):
                sp.dma_start(vblocks[b].rearrange("m r c -> (m r) c").rearrange("(p q) c -> p (q c)", p=S),
                             zeros).then_inc(zero_stored, 16)
            sp.wait_ge(zero_stored, 32)
            for b in range(B):
                sp.wait_ge(v_made, b + 1)
                src = vsb[:, b, :].rearrange("k (m h d) -> k m h d", m=KC, h=HG)
                dst = vblocks[b].rearrange("m (h k) c -> k m h c", h=HG)
                for h in range(HG):
                    sp.dma_start(dst[:, :, h, h * DH:(h + 1) * DH], src[:, :, h, :]).then_inc(v_stored, 16)
            sp.wait_ge(v_stored, B * HG * 16)
            for b in range(B):
                for c in range(3):
                    r0 = 1 if c == 2 else 0
                    sp.dma_start(vblock[r0:CH, b, :, c, :],
                                 vblocks[b][:, CHUNK0[c] + r0:CHUNK0[c] + CH, :].rearrange("m r c -> r m c"))\
                      .then_inc(vblock_loaded, 16)

            def step(s):
                if s.c >= 0 and s.back(-4).exists():
                    load_x(s.back(-4))
                t = s.back(2)
                if t.exists():
                    j = t.c % 2
                    after(sp, x2_done, t.count(1, 1))
                    sp.dma_start(out_v[t.batch(), t.row()], x2[:, j, :]).then_inc(x2_stored[j], 16)
                    after(sp, x2h_done, t.count(1, 1))
                    sp.dma_start(xn2_v[t.batch(), t.row()], x2h[:, j, :]).then_inc(x2h_stored[j], 16)

            steps(sp, step)
            for j in range(2):
                sp.wait_ge(x2_stored[j], 16 * (TILES // 2))
                sp.wait_ge(x2h_stored[j], 16 * (TILES // 2))

        @block.gpsimd
        def _(pool):
            pool.memset(ident[:], 0.0).then_inc(ident_made, 1)
            pool.memset(minus_half[:], -0.5).then_inc(consts_made, 1)
            pool.memset(zeros, 0.0).then_inc(consts_made, 1)
            pool.memset(kblock[:], 0.0).then_inc(consts_made, 1)
            pool.memset(rwT[:], 0.0).then_inc(consts_made, 1)
            pool.wait_ge(ident_made, 1)
            pool.affine_select(out=ident[:], in_=ident[:], compare_op=ALU.not_equal, fill=1.0, base=0,
                               pattern=[[-1, P]], channel_multiplier=1).then_inc(ident_made, 1)
            pool.wait_ge(consts_made, 4)
            pool.wait_ge(ld_small, SMALL)

            def normed(t):
                j = t.c % 2
                after(pool, xh_turned, t.count(1, -1))
                after(pool, ve1_done, t.count(1, 1))
                pool.tensor_tensor(rs1[:, j, :], ve1[:, j, :], minus_half[:], ALU.pow).then_inc(rs1_done, 1)
                after_apart(pool, rs1_done, t.count(1, 1), consts_made, 4)
                pool.tensor_scalar(xh[:, j, :], xs[:, t.c % 4, :], mv1[:, j, 0:1], rs1[:, j, :],
                                   ALU.subtract, ALU.mult).then_inc(xh_done, 1)

            def residual(t):
                after(pool, x2_done, t.count(1, -3))
                pool.tensor_tensor(xb[:, t.c % 4, :], xs[:, t.c % 4, :], bo_sb[:], ALU.add).then_inc(xb_done, 1)

            normed(Tile(0, 0))
            normed(Tile(0, 1))

            def step(s):
                if s.c > FIRST and s.back(-2).exists():
                    normed(s.back(-2))
                t = s.back(2)
                if t.exists():
                    j = t.c % 2
                    after(pool, x2h_done, t.count(1, -1))
                    after(pool, ve2_done, t.count(1, 1))
                    pool.tensor_tensor(rs2[:, j, :], ve2[:, j, :], minus_half[:], ALU.pow).then_inc(rs2_done, 1)
                if s.back(-1).exists():
                    residual(s.back(-1))
                t = s.back(-1)
                if t.exists():
                    after(pool, q_hi_made, t.count(1, 1))
                    pool.tensor_tensor(q_lo[:, t.c % 2], qT[:], q_hi[:, t.c % 2].bitcast(f32),
                                       ALU.subtract).then_inc(q_lo_made, 1)
                if s.c == 0 and isinstance(s.k, int):
                    pool.wait_ge(wo_hi_made, 1)
                    pool.tensor_tensor(wo_lo[:], wo[:], wo_hi[:].bitcast(f32), ALU.subtract).then_inc(wo_lo_made, 1)

            steps(pool, step)

        @block.scalar
        def _(act):
            act.dma_start(en[:], energy.rearrange("b s f -> s b f")).then_inc(ld_en, 16)
            with nc.allow_non_contiguous_dma(reason="biases, once"):
                act.dma_start(bq_sb[:], bq.rearrange("(m p) -> p m", p=P)).then_inc(ld_small, 16)
                act.dma_start(bk_sb[:], bk.rearrange("(m p) -> p m", p=P)).then_inc(ld_small, 16)
            act.dma_start(bv_sb[:], bv.partition_broadcast(S)).then_inc(ld_small, 16)
            act.dma_start(bo_sb[:], bo.partition_broadcast(P)).then_inc(ld_small, 16)
            act.dma_start(rw[:], router_w).then_inc(ld_small, 16)
            for b in range(B):
                act.wait_ge(ctx_turned, b + 1)
                act.activation(ctxT[:, :, b, :], bank[b][:, 0:KC * S].rearrange("p (k s) -> p k s", k=KC),
                               ACT.Copy).then_inc(ctxT_made, 1)
            act.wait_ge(ctx_turned, 3)
            act.wait_ge(consts_made, 4)
            act.activation(rwT[:, :, 0:E], b6[:, 0:KC * E].rearrange("p (k e) -> p k e", k=KC),
                           ACT.Copy).then_inc(ctxT_made, 1)
            for b in range(B):
                act.wait_ge(kblock_made, (b + 1) * HG)
                act.activation(k_hi[:, b], kblock[:, b], ACT.Copy).then_inc(k_hi_made, 1)

            def step(s):
                t = s.back(-1)
                if t.exists():
                    after(act, xh_turned, t.count(1, 1))
                    act.activation(xT[:, t.c % 2], b4[:].rearrange("p (k n) -> p k n", k=KC),
                                   ACT.Copy).then_inc(xT_made, 1)
                t = s.back(3)
                if t.exists():
                    after(act, x2h_turned, t.count(1, 1))
                    act.activation(x2T[:], b5[:].rearrange("p (k n) -> p k n", k=KC),
                                   ACT.Copy).then_inc(x2T_made, 1)
                t = s.back(1)
                if t.exists():
                    if t.c == 0 and isinstance(t.k, int):
                        act.wait_ge(zero_stored, 32)
                    for q in range(3):
                        after(act, probs_turned, t.count(3, q + 1))
                        act.activation(pT[:, t.c % 2, :, q, :],
                                       [b6, b7, b4][q][0:CH, :].rearrange("p (m n) -> p m n", m=KC),
                                       ACT.Copy).then_inc(pT_made, 1)
                if s.exists():
                    after(act, shifted, s.count(1, 1))
                    act.activation(probs[:, s.c % 2], probs[:, s.c % 2], ACT.Exp).then_inc(exp_done, 1)
                t = s.back(-1)
                if t.exists():
                    after(act, qT_made, t.count(1, 1))
                    act.activation(q_hi[:, t.c % 2], qT[:], ACT.Copy).then_inc(q_hi_made, 1)
                t = s.back(1)
                if t.exists():
                    after(act, av_product, t.count(1, 1))
                    act.activation(o_hi[:, t.c % 2], b7[:].rearrange("p (m n) -> p m n", m=KC),
                                   ACT.Copy).then_inc(o_hi_made, 1)
                if s.c == 0 and isinstance(s.k, int):
                    act.wait_ge(ld_wo, 16)
                    act.activation(wo_hi[:], wo[:], ACT.Copy).then_inc(wo_hi_made, 1)

            steps(act, step)

        @block.vector
        def _(dve):
            dve.memset(vblock[0:1, :, :, 2, :], 0.0).then_inc(vblock_ready, 1)
            dve.wait_ge(ld_en, 16)
            dve.tensor_reduce(esum[:], en[:], AX.X, ALU.add, apply_absolute_value=True).then_inc(gate_step, 1)
            dve.wait_ge(gate_step, 1)
            dve.tensor_scalar(ewide[:], esum[:].unsqueeze(2).to_broadcast([S, B, P]), 1.0 / NF, None,
                              ALU.mult).then_inc(gate_step, 1)
            dve.wait_ge(energy_turned, 1)
            energies = b7[:, 0:B * S].rearrange("p (b s) -> p b s", b=B)
            dve.tensor_reduce(emax[:], energies, AX.X, ALU.max).then_inc(gate_step, 1)
            dve.wait_ge(gate_step, 3)
            dve.tensor_scalar(emax[:], emax[:], 1e-8, None, ALU.add).then_inc(gate_step, 1)
            dve.wait_ge(gate_step, 4)
            dve.reciprocal(emax[:], emax[:]).then_inc(gate_step, 1)
            dve.wait_ge(gate_step, 5)
            dve.tensor_tensor(ek[:], energies, emax[:].to_broadcast([P, B, S]), ALU.mult).then_inc(gate_step, 1)
            dve.wait_ge(gate_step, 6)
            dve.tensor_scalar(gate[:], ek[:], THRESHOLD, 0.9, ALU.is_gt, ALU.mult).then_inc(gate_step, 1)
            dve.wait_ge(gate_step, 7)
            dve.tensor_scalar(gate[:], gate[:], 0.1, float(DH) ** -0.5, ALU.add, ALU.mult).then_inc(gate_step, 1)

            def stats(src, st, mv, ve, j, st_done, mv_done, ve_done, t):
                dve.bn_stats(st[:], src).then_inc(st_done, 1)
                after_apart(dve, st_done, t.count(1, 1), x_loaded[0], 16)
                dve.bn_aggr(mv[:, j, :], st[:]).then_inc(mv_done, 1)
                after(dve, mv_done, t.count(1, 1))
                dve.tensor_scalar(ve[:, j, :], mv[:, j, 1:2], ES, None, ALU.add).then_inc(ve_done, 1)

            def stats1(t):
                after(dve, x_loaded[t.c % 4], t.quarters(16, 16))
                after(dve, xh_done, t.count(1, -1))
                stats(xs[:, t.c % 4, :], st1, mv1, ve1, t.c % 2, st1_done, mv1_done, ve1_done, t)

            stats1(Tile(0, 0))
            stats1(Tile(0, 1))
            dve.wait_ge(ld_small, SMALL)
            dve.wait_ge(consts_made, 4)
            for j in range(2):
                dve.wait_ge(kv_product, j + 1)
                dve.tensor_tensor(kT[:, :, 2 * j:2 * j + 2, :],
                                  bank[j][:, 0:2 * B * S].rearrange("p (m b s) -> p b m s", m=2, b=B),
                                  bk_sb[:, 2 * j:2 * j + 2].unsqueeze(1).unsqueeze(3).to_broadcast([P, B, 2, S]),
                                  ALU.add).then_inc(gate_step, 1)
            dve.wait_ge(gate_step, 10)
            for b in range(B):
                for h in range(HG):
                    r = slice(h * DH, (h + 1) * DH)
                    dve.tensor_tensor(kblock[r, b, :, h * S:(h + 1) * S], kT[r, b],
                                      gate[r, b, :].unsqueeze(1).to_broadcast([DH, KC, S]),
                                      ALU.mult).then_inc(kblock_made, 1)
            for b in range(B):
                dve.wait_ge(k_hi_made, b + 1)
                dve.tensor_tensor(k_lo[:, b], kblock[:, b], k_hi[:, b].bitcast(f32), ALU.subtract)\
                   .then_inc(k_lo_made, 1)
            for b in range(B):
                dve.wait_ge(kv_product, 3 + b)
                dve.tensor_tensor(vsb[:, b, :], ps_s[0:S, b, :], bv_sb[:], ALU.add).then_inc(v_made, 1)

            def copy_logits(t):
                after(dve, logit_product, t.count(1, 1))
                dve.tensor_copy(logits[:, t.batch(), t.row(), :], b4[:, 0:E]).then_inc(logits_copied, 1)

            def step(s):
                if s.exists():
                    sc = ps_s[:, :, 0:GS].rearrange("p m (h k) -> p m h k", h=HG)
                    after(dve, scores_done, s.count(1, 1))
                    dve.tensor_reduce(smax[:].rearrange("p (m h) -> p m h", m=KC), sc, AX.X,
                                      ALU.max).then_inc(max_done, 1)
                    if s.back(3).exists():
                        copy_logits(s.back(3))
                    after(dve, max_done, s.count(1, 1))
                    dve.tensor_tensor(probs[:, s.c % 2].rearrange("p (m h) k -> p m h k", m=KC), sc,
                                      smax[:].rearrange("p (m h) -> p m h", m=KC).unsqueeze(3)
                                      .to_broadcast([P, KC, HG, S]), ALU.subtract).then_inc(shifted, 1)
                t = s.back(3)
                if t.exists() and not s.exists():
                    copy_logits(t)
                if s.c > FIRST and s.back(-2).exists():
                    stats1(s.back(-2))
                t = s.back(2)
                if t.exists():
                    j = t.c % 2
                    after(dve, o_product, t.count(1, 1))
                    after(dve, xb_done, t.count(1, 1))
                    after(dve, x2_stored[j], t.halves(16, 0))
                    after(dve, x2h_done, t.count(1, -1))
                    dve.tensor_tensor(x2[:, j, :], b5[:], xb[:, t.c % 4, :], ALU.add).then_inc(x2_done, 1)
                    after(dve, x2_done, t.count(1, 1))
                    stats(x2[:, j, :], st2, mv2, ve2, j, st2_done, mv2_done, ve2_done, t)
                if s.exists():
                    after(dve, exp_done, s.count(1, 1))
                    dve.tensor_reduce(ssum[:], probs[:, s.c % 2], AX.X, ALU.add).then_inc(sum_done, 1)
                    after(dve, sum_done, s.count(1, 1))
                    dve.reciprocal(srec[:], ssum[:]).then_inc(rec_done, 1)
                    after(dve, rec_done, s.count(1, 1))
                    dve.tensor_scalar(sinv[:], srec[:], 0.0, None, ALU.max).then_inc(inv_done, 1)
                t = s.back(-1)
                if t.exists():
                    after(dve, q_product, t.count(1, 1))
                    after(dve, q_lo_made, t.count(1, 0))
                    dve.tensor_tensor(qT[:], b6[:].rearrange("p (m n) -> p m n", m=KC),
                                      bq_sb[:].unsqueeze(2).to_broadcast([P, KC, P]), ALU.add)\
                       .then_inc(qT_made, 1)
                t = s.back(2)
                if t.exists():
                    j = t.c % 2
                    after(dve, x2h_stored[j], t.halves(16, 0))
                    after_apart(dve, rs2_done, t.count(1, 1), x_loaded[0], 16)
                    dve.tensor_scalar(x2h[:, j, :], x2[:, j, :], mv2[:, j, 0:1], rs2[:, j, :],
                                      ALU.subtract, ALU.mult).then_inc(x2h_done, 1)
                if s.exists():
                    after(dve, inv_done, s.count(1, 1))
                    dve.scalar_tensor_tensor(probs[:, s.c % 2], probs[:, s.c % 2], 0.0,
                                             sinv[:].unsqueeze(2).to_broadcast([P, H, S]),
                                             ALU.max, ALU.mult).then_inc(probs_done, 1)
                t = s.back(1)
                if t.exists():
                    after(dve, o_hi_made, t.count(1, 1))
                    dve.tensor_tensor(o_lo[:, t.c % 2], b7[:].rearrange("p (m n) -> p m n", m=KC),
                                      o_hi[:, t.c % 2].bitcast(f32), ALU.subtract).then_inc(o_lo_made, 1)

            steps(dve, step)

        @block.tensor
        def _(pe):
            pe.wait_ge(ident_made, 2)
            pe.wait_ge(ld_ctx, 16)
            for b in range(B):
                for k in range(KC):
                    last = pe.transpose(bank[b][:, k * S:(k + 1) * S], ctx_sb[:, b, k * P:(k + 1) * P],
                                        ident[0:S, 0:S])
                last.then_inc(ctx_turned, 1)
            pe.wait_ge(gate_step, 2)
            for b in range(B):
                last = pe.transpose(b7[:, b * S:(b + 1) * S], ewide[:, b, :], ident[0:S, 0:S])
            last.then_inc(energy_turned, 1)
            pe.wait_ge(ld_wk, 16)
            pe.wait_ge(ctxT_made, 2)
            for m in range(KC):
                for k in range(KC):
                    last = pe.matmul(bank[m // 2][:, m % 2 * B * S:(m % 2 + 1) * B * S], wk[:, k, m * P:(m + 1) * P],
                                     ctxT[:, k].rearrange("p b s -> p (b s)"), start=(k == 0), stop=(k == KC - 1))
                if m % 2:
                    last.then_inc(kv_product, 1)
            pe.wait_ge(ld_wv, 16)
            for b in range(B):
                for k in range(KC):
                    last = pe.matmul(ps_s[0:S, b, :], ctxT[:, k, b, :], wv[:, k, :],
                                     start=(k == 0), stop=(k == KC - 1))
                last.then_inc(kv_product, 1)
            pe.wait_ge(ld_small, SMALL)
            for k in range(KC):
                last = pe.transpose(b6[:, k * E:(k + 1) * E], rw[:, k * P:(k + 1) * P], ident[0:E, 0:E])
            last.then_inc(ctx_turned, 1)
            pe.wait_ge(ld_wq, 16)
            pe.wait_ge(gate_step, 10)
            pe.wait_ge(ctxT_made, 3)

            def step(s):
                t = s.back(-1)
                if t.exists():
                    after(pe, xh_done, t.count(1, 1))
                    after(pe, pT_made, s.back(2).count(3, 3))
                    after(pe, logits_copied, s.back(4).count(1, 1))
                    for k in range(KC):
                        last = pe.transpose(b4[:, k * P:(k + 1) * P], xh[:, t.c % 2, k * P:(k + 1) * P], ident[:])
                    last.then_inc(xh_turned, 1)
                t = s.back(3)
                if t.exists():
                    after(pe, x2h_done, t.count(1, 1))
                    for k in range(KC):
                        last = pe.transpose(b5[:, k * P:(k + 1) * P], x2h[:, t.c % 2, k * P:(k + 1) * P], ident[:])
                    last.then_inc(x2h_turned, 1)
                if s.exists():
                    if s.c == 0 and isinstance(s.k, int):
                        pe.wait_ge(k_lo_made, B)
                        pe.wait_ge(v_made, B)
                    after(pe, q_lo_made, s.count(1, 1))
                    after(pe, shifted, s.count(1, 0))
                    j, b = s.c % 2, s.batch()
                    for m in range(KC):
                        for i, (q, k) in enumerate(PARTS):
                            last = pe.matmul(ps_s[:, m, 0:GS], (q_hi, q_lo)[q][:, j, m, :],
                                             (k_hi, k_lo)[k][:, b, m, :], start=(i == 0), stop=(i == 2))
                    last.then_inc(scores_done, 1)
                t = s.back(3)
                if t.exists():
                    after(pe, x2T_made, t.count(1, 1))
                    after(pe, xT_made, min_tile(s.back(-1)))
                    for k in range(KC):
                        last = pe.matmul(b4[:, 0:RN], x2T[:, k, :], rwT[:, k, :], start=(k == 0), stop=(k == KC - 1))
                    last.then_inc(logit_product, 1)
                t = s.back(1)
                if t.exists():
                    j = t.c % 2
                    after(pe, probs_done, t.count(1, 1))
                    flat = probs[:, j].rearrange("p h k -> p (h k)")
                    for q in range(3):
                        if q == 1:
                            after(pe, o_lo_made, t.count(1, 0))
                        if q == 2:
                            after(pe, xT_made, min_tile(s.back(-1)))
                            after(pe, logits_copied, s.back(3).count(1, 1))
                        for m in range(KC):
                            c0 = m * GS + CHUNK0[q]
                            last = pe.transpose([b6, b7, b4][q][0:CH, m * P:(m + 1) * P],
                                                flat[:, c0:c0 + CH], ident[:])
                        last.then_inc(probs_turned, 1)
                t = s.back(2)
                if t.exists():
                    if t.c == 0 and isinstance(t.k, int):
                        pe.wait_ge(wo_lo_made, 1)
                    j = t.c % 2
                    after(pe, o_lo_made, t.count(1, 1))
                    if s.back(3).exists():
                        after(pe, x2T_made, s.back(3).count(1, 1))
                    for m in range(KC):
                        for i, (a, w) in enumerate(PARTS):
                            last = pe.matmul(b5[:], (o_hi, o_lo)[a][:, j, m, :], (wo_hi, wo_lo)[w][:, m, :],
                                             start=(m == 0 and i == 0), stop=(m == KC - 1 and i == 2))
                    last.then_inc(o_product, 1)
                t = s.back(-1)
                if t.exists():
                    j = t.c % 2
                    after(pe, xT_made, t.count(1, 1))
                    if s.back(1).exists():
                        after(pe, pT_made, s.back(1).count(3, 1))
                    for m in range(KC):
                        for k in range(KC):
                            last = pe.matmul(b6[:, m * P:(m + 1) * P], wq[:, k, m * P:(m + 1) * P],
                                             xT[:, j, k, :], start=(k == 0), stop=(k == KC - 1))
                    last.then_inc(q_product, 1)
                t = s.back(1)
                if t.exists():
                    j, b = t.c % 2, t.batch()
                    if t.c == 0 and isinstance(t.k, int):
                        pe.wait_ge(vblock_ready, 1)
                        pe.wait_ge(vblock_loaded, B * 3 * 16)
                    after(pe, pT_made, t.count(3, 3))
                    for m in range(KC):
                        for q in range(3):
                            last = pe.matmul(b7[:, m * P:(m + 1) * P], vblock[:, b, m, q, :], pT[:, j, m, q, :],
                                             start=(q == 0), stop=(q == 2))
                    last.then_inc(av_product, 1)

            def min_tile(t):
                return t.count(1, 1) if t.exists() else TILES

            steps(pe, step)


def experts(nc, ctx, logits, wg, wu, wd, out, xn2):

    def sb(name, shape, dt=f32):
        return ctx.enter_context(nc.sbuf_tensor(name, shape, dt))

    def sem(name):
        return ctx.enter_context(nc.semaphore(name))

    lt = logits[:].rearrange("p b r e -> p (b r) e")
    T32 = TILES
    pr = sb("pr", [P, T32, E])
    wa = sb("wa", [P, T32, E])
    wb = sb("wb", [P, T32, E])
    oh1 = sb("oh1", [P, T32, E])
    oh2 = sb("oh2", [P, T32, E])
    r1, r2, r3, r4 = (sb(f"r{i}", [P, T32]) for i in range(1, 5))
    rev = sb("rev", [P, E])
    ident = sb("ident2", [P, P])
    same = sb("same", [P, P])
    before = sb("before", [P, P])
    wt = sb("wt", [P, 2, E, SEG])
    key = sb("key", [P, 2 * P])
    gt, eq, eqv, scan, keep, posm = (sb(n, [P, 2 * P]) for n in ("gt", "eq", "eqv", "scan", "keep", "posm"))
    zrow = sb("zrow", [P, 2 * P])
    thr, unit, pick = (sb(n, [P, 1], i32) for n in ("thr", "unit", "pick"))
    cand, digits, picks = (sb(n, [P, 3], i32) for n in ("cand", "digits", "picks"))
    cnt3 = sb("cnt3", [P, 3], bf16)
    same_b = sb("same_b", [P, P], bf16)
    posi = sb("posi", [P, E, SEG, 2], i32)
    pick_f, cgt, ceq, off, ned, ckp = (sb(n, [P, 1]) for n in ("pick_f", "cgt", "ceq", "off", "ned", "ckp"))
    pos = sb("pos", [P, 2, E, SEG])
    hi_ = sb("hi_", [P, E, SEG, 2], i32)
    lo_ = sb("lo_", [P, E, SEG, 2], i32)
    rem = sb("rem", [P, E, SEG, 2])
    rem2 = sb("rem2", [P, E, SEG, 2])
    vals = sb("vals", [P, E, T32, NV], bf16)
    iota_p = sb("iota_p", [P, P], i32)
    iota_c = sb("iota_c", [P, CT], i32)
    hot = sb("hot", [P, T32, P], bf16)
    jhot = sb("jhot", [P, T32, CT], bf16)
    vhot = sb("vhot", [P, T32, CT, NV], bf16)
    lst = sb("lst", [P, CT, NV])
    lid = sb("lid", [P, CT])
    lid2 = sb("lid2", [P, CT])
    lw = sb("lw", [P, CT])
    gidx = sb("gidx", [P, CT], i32)
    sidx_next, sidx = sb("sidx_next", [P, CT], i32), sb("sidx", [P, CT], i32)
    wslot_next, wslot = sb("wslot_next", [P, CT]), sb("wslot", [P, CT])
    xg = sb("xg", [P, CT, D])
    xT_hi = sb("xT_hi", [P, KC, CAP], f32r)
    xT_lo = sb("xT_lo", [P, KC, CAP], f32r)
    raw_gu = sb("raw_gu", [P, 2, 2, KC, 2 * P])
    raw_d = sb("raw_d", [P, 2, 2, D])
    gu_hi = sb("gu_hi", [P, 2, 2, KC, P], f32r)
    gu_lo = sb("gu_lo", [P, 2, 2, KC, P], f32r)
    d_hi = sb("d_hi", [P, 2, D], f32r)
    d_lo = sb("d_lo", [P, 2, D], f32r)
    sil = sb("sil", [P, CAP])
    hid = sb("hid", [P, CAP])
    h_hi = sb("h_hi", [P, 2, CAP], f32r)
    h_lo = sb("h_lo", [P, 2, CAP], f32r)
    ys = sb("ys", [P, CT, D])

    y = [ctx.enter_context(nc.psum_tensor(f"y{i}", [P, D], f32)) for i in range(CT)]
    ga = ctx.enter_context(nc.psum_tensor("ga", [P, 512], f32))
    gb = ctx.enter_context(nc.psum_tensor("gb", [P, 512], f32))
    ub = ctx.enter_context(nc.psum_tensor("ub", [P, 512], f32))

    consts, rev_made = sem("consts"), sem("rev_made")
    chain = sem("chain")
    shift_done, probs_exp = sem("shift_done"), sem("probs_exp")
    wt_done, wt_turned, key_done = sem("wt_done"), sem("wt_turned"), sem("key_done")
    counted, totalled, cand_done, picked, thr_done, unit_done = (
        sem("counted"), sem("totalled"), sem("cand_done"), sem("picked"), sem("thr_done"), sem("unit_done"))
    reached, digits_made, digits_done, split_step, values_done = (
        sem("reached"), sem("digits_made"), sem("digits_done"), sem("split_step"), sem("values_done"))
    tallied, tally_sum, kept, kept_sum, posm_done, pos_turned = (
        sem("tallied"), sem("tally_sum"), sem("kept"), sem("kept_sum"), sem("posm_done"), sem("pos_turned"))
    slots_done = sem("slots_done")
    hot_done, jhot_done, vhot_done, list_product, list_read, list_made = (
        sem("hot_done"), sem("jhot_done"), sem("vhot_done"), sem("list_product"), sem("list_read"), sem("list_made"))
    list_step, slots_listed = sem("list_step"), sem("slots_listed")
    gathered, xg_turned, xT_hi_done, xT_lo_done = (
        [sem(f"gathered{t}") for t in range(CT)], sem("xg_turned"), sem("xT_hi_done"), sem("xT_lo_done"))
    gu_loaded = [sem(f"gu_loaded{i}") for i in range(2)]
    d_loaded = [sem(f"d_loaded{i}") for i in range(2)]
    gu_hi_done, gu_lo_done, d_hi_done, d_lo_done = (
        sem("gu_hi_done"), sem("gu_lo_done"), sem("d_hi_done"), sem("d_lo_done"))
    a_product, gb_product, ub_product, y_product = (
        sem("a_product"), sem("gb_product"), sem("ub_product"), sem("y_product"))
    sil_done, hid_done, h_hi_done, h_lo_done = sem("sil_done"), sem("hid_done"), sem("h_hi_done"), sem("h_lo_done")
    ys_act, ys_dve, scattered, slots_moved = sem("ys_act"), sem("ys_dve"), sem("scattered"), sem("slots_moved")

    wg_v = wg.rearrange("e (k p) (q f) -> e q p k f", p=P, f=2 * P)
    wu_v = wu.rearrange("e (k p) (q f) -> e q p k f", p=P, f=2 * P)
    wd_v = wd.rearrange("e (q c p) d -> e q p c d", p=P, c=2)
    out_rows = out.rearrange("b l d -> (b l) d")
    PAIRS = FC // 2

    def make_values(eng, e):
        after(eng, list_product, e)
        eng.tensor_tensor(jhot[:], iota_c[:].unsqueeze(1).to_broadcast([P, T32, CT]),
                          hi_[:, e].rearrange("p s two -> p (s two)").unsqueeze(2).to_broadcast([P, T32, CT]),
                          ALU.is_equal).then_inc(jhot_done, 1)
        after(eng, jhot_done, e + 1)
        eng.tensor_tensor(vhot[:], jhot[:].unsqueeze(3).to_broadcast([P, T32, CT, NV]),
                          vals[:, e].unsqueeze(2).to_broadcast([P, T32, CT, NV]),
                          ALU.mult).then_inc(vhot_done, 1)

    def make_hots(eng, e, piece):
        place = lo_[:, e].rearrange("p s two -> p (s two)")[:, bass.ds(piece * HOT, HOT)]
        eng.tensor_tensor(hot[:, bass.ds(piece * HOT, HOT), :], iota_p[:].unsqueeze(1).to_broadcast([P, HOT, P]),
                          place.unsqueeze(2).to_broadcast([P, HOT, P]), ALU.is_equal).then_inc(hot_done, 1)

    class Chunk:

        def __init__(self, e, k, c):
            self.e, self.k, self.c = e, k, c

        def count(self, per, extra):
            return self.e * (FC * per) + self.k * (4 * per) + (self.c * per + extra)

        def pairs(self, per, extra):
            return self.e * (FC // 4 * per) + self.k * per + ((self.c // 4) * per + extra)

        def ahead(self, n):
            return Chunk(self.e, self.k, self.c + n)

        def exists(self):
            return not isinstance(self.e, int) or self.e * FC + self.c < E * FC

    def run_chunks(eng, e, chunk):
        chunk(Chunk(e, 0, 0))
        chunk(Chunk(e, 0, 1))
        with eng.Fori(0, (FC - 4) // 4) as k:
            for c in range(2, 6):
                chunk(Chunk(e, k, c))
        chunk(Chunk(e, 0, FC - 2))
        chunk(Chunk(e, 0, FC - 1))

    def run_experts(eng, expert):
        expert(0, True)
        with eng.Fori(1, E - 1) as e:
            expert(e, True)
        expert(E - 1, False)

    with nc.Block() as block:

        @block.sync
        def _(sp):
            def load(e, q, slot, uses):
                after(sp, gu_hi_done, uses(2, 0))
                after(sp, gu_lo_done, uses(2, 0))
                sp.dma_start(raw_gu[:, slot, 0], wg_v[e, q]).then_inc(gu_loaded[slot], 16)
                sp.dma_start(raw_gu[:, slot, 1], wu_v[e, q]).then_inc(gu_loaded[slot], 16)
                after(sp, d_hi_done, uses(2, 0))
                after(sp, d_lo_done, uses(2, 0))
                sp.dma_start(raw_d[:, slot], wd_v[e, q]).then_inc(d_loaded[slot], 16)

            for q in range(2):
                load(0, q, q, lambda per, extra: 0)
            with sp.Fori(0, (PAIRS - 2) // 2) as k:
                for j in range(2):
                    load(0, k * 2 + (2 + j), j, lambda per, extra, j=j: k * 4 + (2 * (2 + j) - 2))
            with sp.Fori(1, E) as e:
                with sp.Fori(0, PAIRS // 2) as k:
                    for j in range(2):
                        load(e, k * 2 + j, j, lambda per, extra, j=j: e * FC + k * 4 + (2 * j - 2))

        @block.gpsimd
        def _(pool):
            pool.iota(rev[:], [[-1, E]], base=E, channel_multiplier=0,
                      allow_small_or_imprecise_dtypes=True).then_inc(rev_made, 1)
            pool.memset(ident[:], 0.0).then_inc(consts, 1)
            pool.memset(same[:], 1.0).then_inc(consts, 1)
            pool.memset(zrow[:], 0.0).then_inc(consts, 1)
            pool.memset(thr[:], 0).then_inc(consts, 1)
            for j in range(3):
                pool.memset(digits[:, j:j + 1], (j + 1) << (BITS - 2)).then_inc(digits_made, 1)
            pool.memset(unit[:], 1 << (BITS - 2)).then_inc(consts, 1)
            pool.iota(iota_p[:], [[1, P]], base=0, channel_multiplier=0,
                      allow_small_or_imprecise_dtypes=True).then_inc(consts, 1)
            pool.iota(iota_c[:], [[1, CT]], base=0, channel_multiplier=0,
                      allow_small_or_imprecise_dtypes=True).then_inc(consts, 1)
            pool.iota(vals[:, :, :, 0], [[0, E], [1, T32]], base=0, channel_multiplier=0,
                      allow_small_or_imprecise_dtypes=True).then_inc(consts, 1)
            pool.iota(vals[:, :, :, 1], [[0, E], [0, T32]], base=0, channel_multiplier=1,
                      allow_small_or_imprecise_dtypes=True).then_inc(consts, 1)
            pool.memset(vals[:, :, :, 2], 1.0).then_inc(consts, 1)
            pool.wait_ge(consts, 10)
            pool.affine_select(out=ident[:], in_=ident[:], compare_op=ALU.not_equal, fill=1.0, base=0,
                               pattern=[[-1, P]], channel_multiplier=1).then_inc(consts, 1)
            pool.affine_select(out=same[:], in_=same[:], compare_op=ALU.is_ge, fill=0.0, base=0,
                               pattern=[[-SEG, E], [0, SEG]], channel_multiplier=1).then_inc(consts, 1)
            pool.wait_ge(consts, 12)
            pool.affine_select(out=same[:], in_=same[:], compare_op=ALU.is_ge, fill=0.0, base=SEG - 1,
                               pattern=[[SEG, E], [0, SEG]], channel_multiplier=-1).then_inc(consts, 1)
            pool.wait_ge(consts, 13)
            pool.tensor_copy(same_b[:], same[:]).then_inc(consts, 1)
            pool.affine_select(out=before[:], in_=same[:], compare_op=ALU.is_gt, fill=0.0, base=0,
                               pattern=[[1, P]], channel_multiplier=-1).then_inc(consts, 1)

            def scatter(e):
                after(pool, scattered, e * (16 * CT))
                after(pool, ys_act, e * 3 + 3)
                after_apart(pool, ys_dve, e * 2 + 2, consts, 15)
                for t in range(CT):
                    pool.indirect_dma_start(
                        out=out_rows, out_offset=bass.IndirectOffsetOnAxis(ap=sidx[:, t:t + 1], axis=0),
                        in_=ys[:, t, :], in_offset=None, bounds_check=N - 1, oob_is_err=False,
                        compute_op=ALU.add).then_inc(scattered, 16)

            def gather(e):
                after(pool, list_made, e + 1)
                after_apart(pool, xg_turned, e * CT, consts, 15)
                for t in range(CT):
                    pool.indirect_dma_start(
                        out=xg[:, t, :], out_offset=None, in_=xn2,
                        in_offset=bass.IndirectOffsetOnAxis(ap=gidx[:, t:t + 1], axis=0),
                        bounds_check=N - 1, oob_is_err=False).then_inc(gathered[t], 16)

            pool.wait_ge(wt_done, 1)
            weights = wt[:].rearrange("p two e s -> p e s two")
            parts = vals[:].rearrange("p e (s two) v -> p e s two v", two=2)
            pool.tensor_copy(parts[:, :, :, :, 3], weights).then_inc(split_step, 1)
            pool.wait_ge(split_step, 1)
            pool.tensor_tensor(rem[:], weights, parts[:, :, :, :, 3], ALU.subtract).then_inc(split_step, 1)
            pool.wait_ge(split_step, 2)
            pool.tensor_copy(parts[:, :, :, :, 4], rem[:]).then_inc(split_step, 1)
            pool.wait_ge(split_step, 3)
            pool.tensor_tensor(rem2[:], rem[:], parts[:, :, :, :, 4], ALU.subtract).then_inc(split_step, 1)
            pool.wait_ge(split_step, 4)
            pool.tensor_copy(parts[:, :, :, :, 5], rem2[:]).then_inc(values_done, 1)
            gather(0)

            def expert(e, more):
                if more:
                    gather(e + 1)
                scatter(e)

            run_experts(pool, expert)
            pool.wait_ge(scattered, 16 * CT * E)

        @block.scalar
        def _(act):
            act.wait_ge(shift_done, 1)
            act.activation(pr[:], pr[:], ACT.Exp).then_inc(probs_exp, 1)

            def split_gu(c):
                if not c.exists():
                    return
                s, pair = c.c % 2, c.c // 2 % 2
                after(act, gu_loaded[pair], c.pairs(32, 32))
                after(act, ub_product, c.count(1, -1))
                act.activation(gu_hi[:, s], raw_gu[:, pair, :, :, s * P:(s + 1) * P],
                               ACT.Copy).then_inc(gu_hi_done, 1)

            def split_d(c):
                if not c.exists():
                    return
                s, pair = c.c % 2, c.c // 2 % 2
                after(act, d_loaded[pair], c.pairs(16, 16))
                after(act, y_product, c.count(1, -1))
                act.activation(d_hi[:, s], raw_d[:, pair, s, :], ACT.Copy).then_inc(d_hi_done, 1)

            def turned(e, tiles):
                for t in tiles:
                    after(act, xg_turned, e * CT + (t + 1))
                    act.activation(xT_hi[:, :, t * P:(t + 1) * P],
                                   [ga, gb, ub][t % 3][:].rearrange("p (k n) -> p k n", k=KC),
                                   ACT.Copy).then_inc(xT_hi_done, 1)

            split_gu(Chunk(0, 0, 0))
            split_gu(Chunk(0, 0, 1))
            split_d(Chunk(0, 0, 0))
            turned(0, range(CT))

            def expert(e, more):
                def chunk(c):
                    s = c.c % 2
                    after(act, a_product, c.count(1, 1))
                    after(act, hid_done, c.count(2, 0))
                    act.activation(sil[:, 0:NA], ga[:, 0:NA], ACT.Silu).then_inc(sil_done, 1)
                    after(act, gb_product, c.count(1, 1))
                    act.activation(sil[:, NA:CAP], gb[:, 0:NB], ACT.Silu).then_inc(sil_done, 1)
                    if c.c == FC - 1 and more:
                        turned(e + 1, range(1))
                    split_gu(c.ahead(2))
                    after(act, hid_done, c.count(2, 2))
                    act.activation(h_hi[:, s, :], hid[:], ACT.Copy).then_inc(h_hi_done, 1)
                    split_d(c.ahead(1))

                run_chunks(act, e, chunk)
                if more:
                    turned(e + 1, range(1, CT))
                after(act, y_product, e * FC + FC)
                after(act, slots_moved, e * 2 + 2)
                after(act, scattered, e * (16 * CT))
                for t in range(3):
                    act.activation(ys[:, t, :], y[t][:], ACT.Copy, scale=wslot[:, t:t + 1]).then_inc(ys_act, 1)

            run_experts(act, expert)

        @block.vector
        def _(dve):
            n = [0]

            def link(ins):
                n[0] += 1
                ins.then_inc(chain, 1)
                dve.wait_ge(chain, n[0])

            def over_e(a):
                return a[:].unsqueeze(2).to_broadcast([P, T32, E])

            link(dve.tensor_reduce(r1[:], lt, AX.X, ALU.max))
            dve.tensor_tensor(pr[:], lt, over_e(r1), ALU.subtract).then_inc(shift_done, 1)
            dve.wait_ge(probs_exp, 1)
            link(dve.tensor_reduce(r2[:], pr[:], AX.X, ALU.add))
            link(dve.reciprocal(r3[:], r2[:]))
            link(dve.tensor_tensor(pr[:], pr[:], over_e(r3), ALU.mult))
            dve.wait_ge(rev_made, 1)
            rev_b = rev[:].unsqueeze(1).to_broadcast([P, T32, E])

            def first_max(src, top, one_hot):
                link(dve.tensor_reduce(top[:], src[:], AX.X, ALU.max))
                link(dve.tensor_tensor(wa[:], src[:], over_e(top), ALU.is_equal))
                link(dve.tensor_tensor(wa[:], wa[:], rev_b, ALU.mult))
                link(dve.tensor_reduce(r4[:], wa[:], AX.X, ALU.max))
                link(dve.tensor_tensor(one_hot[:], wa[:], over_e(r4), ALU.is_equal))

            first_max(pr, r1, oh1)
            link(dve.scalar_tensor_tensor(wb[:], oh1[:], -2.0, pr[:], ALU.mult, ALU.add))
            first_max(wb, r2, oh2)
            link(dve.tensor_tensor(r3[:], r1[:], r2[:], ALU.add))
            link(dve.tensor_scalar(r3[:], r3[:], 1e-6, None, ALU.add))
            link(dve.reciprocal(r3[:], r3[:]))
            link(dve.tensor_tensor(r1[:], r1[:], r3[:], ALU.mult))
            link(dve.tensor_tensor(r2[:], r2[:], r3[:], ALU.mult))
            link(dve.tensor_tensor(wa[:], oh1[:], over_e(r1), ALU.mult))
            link(dve.tensor_tensor(wb[:], oh2[:], over_e(r2), ALU.mult))
            sep = "p (s two) e -> p s two e"
            dve.tensor_tensor(wt[:].rearrange("p two e s -> p s two e"), wa[:].rearrange(sep, two=2),
                              wb[:].rearrange(sep, two=2), ALU.add).then_inc(wt_done, 1)
            dve.wait_ge(wt_turned, 1)
            dve.tensor_copy(key[:], ga[:, 0:2 * P]).then_inc(key_done, 1)
            dve.wait_ge(key_done, 1)

            dve.wait_ge(digits_made, 3)
            dve.wait_ge(consts, 15)
            with dve.Fori(0, PAIRS_OF_BITS // SEARCH) as turn:
                for u in range(SEARCH):
                    done = turn * SEARCH + (u + 1)
                    dve.tensor_tensor(cand[:], thr[:].to_broadcast([P, 3]), digits[:], ALU.bitwise_or)\
                       .then_inc(cand_done, 1)
                    dve.wait_ge(cand_done, done)
                    for j in range(3):
                        dve.tensor_scalar((eq, eqv, scan)[j][:], key[:], cand[:, j:j + 1].bitcast(f32), 0.0, ALU.is_ge, ALU.add,
                                          accum_out=cnt3[:, j:j + 1]).then_inc(counted, 1)
                    dve.tensor_scalar(digits[:], digits[:], 2, None, ALU.logical_shift_right).then_inc(digits_done, 1)
                    dve.wait_ge(totalled, done)
                    dve.scalar_tensor_tensor(picks[:], gb[:, 0:3], float(CAP), unit[:].to_broadcast([P, 3]),
                                             ALU.is_ge, ALU.mult, accum_out=pick_f[:]).then_inc(reached, 1)
                    dve.wait_ge(reached, done)
                    dve.tensor_copy(pick[:], pick_f[:]).then_inc(picked, 1)
                    dve.wait_ge(picked, done)
                    dve.tensor_tensor(thr[:], thr[:], pick[:], ALU.bitwise_or).then_inc(thr_done, 1)
                    dve.tensor_scalar(unit[:], unit[:], 2, None, ALU.logical_shift_right).then_inc(unit_done, 1)
                    dve.wait_ge(thr_done, done)
                    dve.wait_ge(unit_done, done)
                    dve.wait_ge(digits_done, done)

            thr_f = thr[:].bitcast(f32)
            dve.tensor_scalar(gt[:], key[:], thr_f, 0.0, ALU.is_gt, ALU.add, accum_out=cgt[:]).then_inc(tallied, 1)
            link(dve.tensor_scalar(eq[:], key[:], thr_f, None, ALU.is_equal))
            dve.scalar_tensor_tensor(eqv[:], key[:], 0.0, eq[:], ALU.is_gt, ALU.mult,
                                     accum_out=ceq[:]).then_inc(tallied, 1)
            dve.wait_ge(tallied, 2)
            dve.wait_ge(tally_sum, 1)
            link(dve.tensor_scalar(ned[:], gb[:, 0:1], -1.0, float(CAP), ALU.mult, ALU.add))
            link(dve.tensor_copy(off[:], gb[:, 1:2]))
            link(dve.tensor_tensor_scan(scan[:], eqv[:], zrow[:], off[:], ALU.add, ALU.add))
            link(dve.tensor_tensor(scan[:], scan[:], eqv[:], ALU.subtract))
            link(dve.scalar_tensor_tensor(eqv[:], scan[:], ned[:], eqv[:], ALU.is_lt, ALU.mult))
            dve.scalar_tensor_tensor(keep[:], gt[:], 1.0, eqv[:], ALU.mult, ALU.add,
                                     accum_out=ckp[:]).then_inc(kept, 1)
            dve.wait_ge(kept, 1)
            dve.wait_ge(kept_sum, 1)
            link(dve.tensor_copy(off[:], gb[:, 0:1]))
            link(dve.tensor_tensor_scan(scan[:], keep[:], zrow[:], off[:], ALU.add, ALU.add))
            link(dve.tensor_tensor(scan[:], scan[:], keep[:], ALU.mult))
            dve.tensor_scalar(posm[:], scan[:], -1.0, None, ALU.add).then_inc(posm_done, 1)
            dve.wait_ge(pos_turned, 1)
            link(dve.tensor_copy(pos[:].rearrange("p two e s -> p (two e s)"), ub[:, 0:2 * P]))
            posv = pos[:].rearrange("p two e s -> p e s two")
            link(dve.tensor_copy(posi[:], posv))
            dve.tensor_scalar(hi_[:], posi[:], TILE_BITS, None, ALU.arith_shift_right).then_inc(slots_done, 1)
            dve.tensor_scalar(lo_[:], posi[:], P - 1, None, ALU.bitwise_and).then_inc(slots_done, 1)
            dve.wait_ge(slots_done, 2)
            dve.wait_ge(values_done, 1)
            make_values(dve, 0)
            for piece in range(4):
                make_hots(dve, 0, piece)

            def read_list(e):
                after(dve, list_product, e + 1)
                dve.tensor_copy(lst[:].rearrange("p c v -> p (c v)"), ga[:, 0:CT * NV]).then_inc(list_read, 1)
                after(dve, list_read, e + 1)
                dve.scalar_tensor_tensor(lid[:], lst[:, :, 0], float(P), lst[:, :, 1], ALU.mult,
                                         ALU.add).then_inc(list_step, 1)
                dve.tensor_tensor(lw[:], lst[:, :, 5], lst[:, :, 4], ALU.add).then_inc(list_step, 1)
                after(dve, list_step, e * 3 + 2)
                dve.scalar_tensor_tensor(lid2[:], lst[:, :, 2], -8192.0, lid[:], ALU.mult,
                                         ALU.add).then_inc(list_step, 1)
                after(dve, list_step, e * 3 + 3)
                dve.tensor_scalar(sidx_next[:], lid2[:], 8192.0, None, ALU.add)\
                   .then_inc(slots_listed, 1)
                dve.tensor_tensor(wslot_next[:], lw[:], lst[:, :, 3], ALU.add).then_inc(slots_listed, 1)
                for t in range(CT):
                    after(dve, gathered[t], e * 16)
                dve.tensor_copy(gidx[:], lid[:]).then_inc(list_made, 1)

            def move_slots(e):
                after(dve, slots_listed, e * 2 + 2)
                after(dve, scattered, e * (16 * CT))
                after(dve, ys_act, e * 3)
                dve.tensor_copy(sidx[:], sidx_next[:]).then_inc(slots_moved, 1)
                dve.tensor_copy(wslot[:], wslot_next[:]).then_inc(slots_moved, 1)
                after(dve, slots_moved, e * 2 + 2)

            def split_gu(c):
                if not c.exists():
                    return
                s, pair = c.c % 2, c.c // 2 % 2
                after(dve, gu_hi_done, c.count(1, 1))
                dve.tensor_tensor(gu_lo[:, s], raw_gu[:, pair, :, :, s * P:(s + 1) * P],
                                  gu_hi[:, s].bitcast(f32), ALU.subtract).then_inc(gu_lo_done, 1)

            def split_d(c):
                if not c.exists():
                    return
                s, pair = c.c % 2, c.c // 2 % 2
                after(dve, d_hi_done, c.count(1, 1))
                dve.tensor_tensor(d_lo[:, s], raw_d[:, pair, s, :], d_hi[:, s].bitcast(f32),
                                  ALU.subtract).then_inc(d_lo_done, 1)

            def turned(e, tiles):
                for t in tiles:
                    after(dve, xT_hi_done, e * CT + (t + 1))
                    part = slice(t * P, (t + 1) * P)
                    dve.tensor_tensor(xT_lo[:, :, part],
                                      [ga, gb, ub][t % 3][:].rearrange("p (k n) -> p k n", k=KC),
                                      xT_hi[:, :, part].bitcast(f32), ALU.subtract).then_inc(xT_lo_done, 1)

            split_gu(Chunk(0, 0, 0))
            split_gu(Chunk(0, 0, 1))
            split_d(Chunk(0, 0, 0))
            read_list(0)
            turned(0, range(CT))

            def expert(e, more):
                def chunk(c):
                    s = c.c % 2
                    if c.c == FC - 2:
                        move_slots(e)
                    after(dve, sil_done, c.count(2, 1))
                    after(dve, h_lo_done, c.count(1, 0))
                    dve.tensor_tensor(hid[:, 0:NA], sil[:, 0:NA], ga[:, NA:2 * NA], ALU.mult).then_inc(hid_done, 1)
                    after(dve, sil_done, c.count(2, 2))
                    after(dve, ub_product, c.count(1, 1))
                    dve.tensor_tensor(hid[:, NA:CAP], sil[:, NA:CAP], ub[:, 0:NB], ALU.mult).then_inc(hid_done, 1)
                    if c.c == FC - 1 and more:
                        turned(e + 1, range(1))
                    split_gu(c.ahead(2))
                    after(dve, h_hi_done, c.count(1, 1))
                    dve.tensor_tensor(h_lo[:, s, :], hid[:], h_hi[:, s, :].bitcast(f32),
                                      ALU.subtract).then_inc(h_lo_done, 1)
                    if c.c == FC - 2 and more:
                        read_list(e + 1)
                    split_d(c.ahead(1))
                    if c.c == 0 and more:
                        make_values(dve, e + 1)
                    if c.c == 1 and more:
                        make_hots(dve, e + 1, 0)
                    if c.c == 4 and more:
                        make_hots(dve, e + 1, c.k + 1)

                run_chunks(dve, e, chunk)
                if more:
                    turned(e + 1, range(1, CT))
                after(dve, y_product, e * FC + FC)
                after(dve, scattered, e * (16 * CT))
                for t in range(3, CT):
                    dve.tensor_scalar(ys[:, t, :], y[t][:], wslot[:, t:t + 1], None, ALU.mult).then_inc(ys_dve, 1)

            run_experts(dve, expert)

        @block.tensor
        def _(pe):
            pe.wait_ge(consts, 15)
            pe.wait_ge(wt_done, 1)
            for two in range(2):
                last = pe.transpose(ga[:, two * P:(two + 1) * P], wt[:, two].rearrange("p e s -> p (e s)"), ident[:])
            last.then_inc(wt_turned, 1)
            with pe.Fori(0, PAIRS_OF_BITS // SEARCH) as turn:
                for u in range(SEARCH):
                    pe.wait_ge(counted, turn * (3 * SEARCH) + (3 * u + 3))
                    pe.matmul(gb[:, 0:3], same_b[:], cnt3[:], start=True, stop=True).then_inc(totalled, 1)
            pe.wait_ge(tallied, 2)
            pe.wait_ge(thr_done, PAIRS_OF_BITS)
            pe.matmul(gb[:, 0:1], same[:], cgt[:], start=True, stop=True)
            pe.matmul(gb[:, 1:2], before[:], ceq[:], start=True, stop=True).then_inc(tally_sum, 1)
            pe.wait_ge(kept, 1)
            pe.matmul(gb[:, 0:1], before[:], ckp[:], start=True, stop=True).then_inc(kept_sum, 1)
            pe.wait_ge(posm_done, 1)
            for two in range(2):
                last = pe.transpose(ub[:, two * P:(two + 1) * P], posm[:, two * P:(two + 1) * P], ident[:])
            last.then_inc(pos_turned, 1)

            def make_list(e):
                after(pe, vhot_done, e + 1)
                for t in range(T32):
                    if t % HOT == 0:
                        after(pe, hot_done, e * 4 + (t // HOT + 1))
                    last = pe.matmul(ga[:, 0:CT * NV], hot[:, t, :], vhot[:, t].rearrange("p c v -> p (c v)"),
                                     start=(t == 0), stop=(t == T32 - 1))
                last.then_inc(list_product, 1)

            def turn(e, t):
                after(pe, gathered[t], e * 16 + 16)
                if t >= 3:
                    after(pe, xT_lo_done, e * CT + (t - 2))
                for k in range(KC):
                    last = pe.transpose([ga, gb, ub][t % 3][:, k * P:(k + 1) * P],
                                        xg[:, t, k * P:(k + 1) * P], ident[:])
                last.then_inc(xg_turned, 1)

            make_list(0)
            pe.wait_ge(list_read, 1)
            for t in range(CT):
                turn(0, t)

            def up(c):
                s = c.c % 2
                w_, x_ = (gu_hi, gu_lo), (xT_hi, xT_lo)
                for bank_, cols, which, t0, n_, sem_ in (
                        (ga, 0, 0, 0, NA, None), (ga, NA, 1, 0, NA, a_product),
                        (gb, 0, 0, NA, NB, gb_product), (ub, 0, 1, NA, NB, ub_product)):
                    for i, (a, b) in enumerate(PARTS):
                        for k in range(KC):
                            last = pe.matmul(bank_[:, cols:cols + n_], w_[a][:, s, which, k, :],
                                             x_[b][:, k, t0:t0 + n_],
                                             start=(i == 0 and k == 0), stop=(i == 2 and k == KC - 1))
                    if sem_ is not None:
                        last.then_inc(sem_, 1)
                    if c.c == 0 and sem_ is a_product:
                        after(pe, xT_lo_done, c.e * CT + CT)

            def down(c, start, stop):
                s = c.c % 2
                after(pe, h_lo_done, c.count(1, 1))
                after(pe, d_lo_done, c.count(1, 1))
                h_, d_ = (h_hi, h_lo), (d_hi, d_lo)
                for t in range(CT):
                    for i, (a, b) in enumerate(PARTS):
                        last = pe.matmul(y[t][:], h_[a][:, s, t * P:(t + 1) * P], d_[b][:, s, :],
                                         start=(start and i == 0), stop=(stop and i == 2))
                last.then_inc(y_product, 1)

            def expert(e, more):
                def chunk(c):
                    after(pe, gu_lo_done, c.count(1, 1))
                    if c.c == 0:
                        after(pe, xT_lo_done, e * CT + 4)
                    else:
                        after(pe, hid_done, c.count(2, 0))
                    if c.c == FC - 1 and more:
                        after(pe, list_read, e + 2)
                    up(c)
                    if c.c == FC - 2 and more:
                        after(pe, hid_done, c.count(2, 1))
                        make_list(e + 1)
                    if c.c == FC - 1 and more:
                        after(pe, hid_done, c.count(2, 1))
                        turn(e + 1, 0)
                    if c.c == 1:
                        after(pe, ys_act, e * 3)
                        after(pe, ys_dve, e * 2)
                    if c.c > 0:
                        down(c.ahead(-1), start=(c.c == 1), stop=False)

                run_chunks(pe, e, chunk)
                last_chunk = Chunk(e, 0, FC - 1)
                if more:
                    after(pe, hid_done, last_chunk.count(2, 2))
                    for t in range(1, 4):
                        turn(e + 1, t)
                down(last_chunk, start=False, stop=True)
                if more:
                    turn(e + 1, 4)

            run_experts(pe, expert)


def build(nc, x, context, energy, Wq, bq, Wk, bk, Wv, bv, Wo, bo, router_w, wg, wu, wd, out):
    xn2 = nc.dram_tensor("xn2", [N, D], f32, kind="Internal").ap()
    vblocks = nc.dram_tensor("vblocks", [B, KC, GS, P], f32, kind="Internal").ap()
    with nc.sbuf_tensor("logits", [P, B, TILES // B, E], f32) as logits:
        with ExitStack() as ctx:
            attention(nc, ctx, x, context, energy, Wq, bq, Wk, bk, Wv, bv, Wo, bo, router_w, out,
                      xn2, vblocks, logits)
        with ExitStack() as ctx:
            experts(nc, ctx, logits, wg, wu, wd, out, xn2)


_INS = ["x", "ctx_1024", "ctxb_2048x32", "L0_xattn_Wq", "L0_xattn_bq", "L0_xattn_Wk", "L0_xattn_bk",
        "L0_xattn_Wv", "L0_xattn_bv", "L0_xattn_Wo", "L0_xattn_bo", "L0_ffn_router_w", "L0_ffn_wg",
        "L0_ffn_wu", "L0_ffn_wd"]
_OUTS = [((B, L, D), "float32")]


def kernel(**inputs):
    import numpy as _np
    import concourse.bacc as _bacc
    from concourse import mybir as _mybir
    from concourse.bass_utils import run_bass_kernel_spmd as _run

    nc = _bacc.Bacc("TRN2", target_bir_lowering=False, num_devices=1)
    arrays, args = {}, []
    for name in _INS:
        a = _np.ascontiguousarray(inputs[name])
        arrays[f"in_{name}_dram"] = a
        args.append(nc.dram_tensor(f"in_{name}_dram", a.shape, _mybir.dt.from_np(a.dtype), kind="ExternalInput").ap())
    for i, (shape, dtype) in enumerate(_OUTS):
        dt = _mybir.dt.from_np(_np.dtype(dtype))
        args.append(nc.dram_tensor(f"out_{i}_dram", shape, dt, kind="ExternalOutput").ap())
    build(nc, *args)
    r = _run(nc, [arrays], core_ids=[0])
    got = tuple(r.results[0][f"out_{i}_dram"] for i in range(len(_OUTS)))
    return got[0]
```

```python
import concourse.bass as bass
from concourse import mybir
from contextlib import ExitStack

f32 = mybir.dt.float32
f32r = mybir.dt.float32r
bf16 = mybir.dt.bfloat16
i32 = mybir.dt.int32
ALU = mybir.AluOpType
ACT = mybir.ActivationFunctionType
AX = mybir.AxisListType

P = 128
B, L, D = 2, 2048, 512
N = B * L
TILES = N // P
H, DH = 16, 32
S = 77
NF = 32
KC = D // P
HG = P // DH
GS = HG * S
CH = 103
CHUNK0 = [0, CH, GS - CH]
E, F, TOPK = 8, 2048, 2
CAP = max(1, int(1.25 * N / E))
CT = CAP // P
NA = 256
NB = CAP - NA
FC = F // P
SEG = 16
NV = 6
ES = 1e-5
BITS = 30
PAIRS_OF_BITS = BITS // 2
HIGH = (BITS - 16) // 2
SEARCH = 4
HOT = TILES // 4
TILE_BITS = P.bit_length() - 1
THRESHOLD = 0.1
RN = 96
PARTS = ((0, 0), (0, 1), (1, 0))


class Tile:

    def __init__(self, k, c):
        self.k, self.c = k, c

    def count(self, per, extra):
        return self.k * (4 * per) + (self.c * per + extra)

    def halves(self, per, extra):
        return self.k * (2 * per) + ((self.c // 2) * per + extra)

    def quarters(self, per, extra):
        return self.k * per + ((self.c // 4) * per + extra)

    def back(self, n):
        return Tile(self.k, self.c - n)

    def exists(self):
        return not isinstance(self.k, int) or 0 <= self.c < TILES

    def batch(self):
        return self.c % 2

    def pair(self):
        return self.c // 2 % 2

    def row(self):
        return self.k * 2 + self.c // 2


def after(eng, sem, n):
    if isinstance(n, int) and n <= 0:
        return
    eng.wait_ge(sem, n)


def after_apart(eng, sem, n, met, value):
    if isinstance(n, int):
        after(eng, sem, n)
        return
    n = eng.compute_val(n)
    eng.wait_ge(met, value)
    eng.wait_ge(sem, n)


FIRST, LOOP, LOOPS, LAST = -3, 4, 6, TILES + 3


def steps(eng, step):
    for c in range(FIRST, LOOP):
        step(Tile(0, c))
    with eng.Fori(0, LOOPS) as k:
        for c in range(LOOP, LOOP + 4):
            step(Tile(k, c))
    for c in range(LOOP + 4 * LOOPS, LAST):
        step(Tile(0, c))


def attention(nc, ctx, x, context, energy, Wq, bq, Wk, bk, Wv, bv, Wo, bo, router_w, out,
              xn2, vblocks, logits):

    def sb(name, shape, dt=f32):
        return ctx.enter_context(nc.sbuf_tensor(name, shape, dt))

    def sem(name):
        return ctx.enter_context(nc.semaphore(name))

    wo_hi = sb("wo_hi", [P, KC, D], f32r)
    wo_lo = sb("wo_lo", [P, KC, D], f32r)
    wq_hi = sb("wq_hi", [P, KC, D], f32r)
    wq_lo = sb("wq_lo", [P, KC, D], f32r)
    wk = sb("wk", [P, KC, D])
    wv = sb("wv", [P, KC, D])
    bq_sb = sb("bq_sb", [P, KC])
    bk_sb = sb("bk_sb", [P, KC])
    bv_sb = sb("bv_sb", [S, D])
    bo_sb = sb("bo_sb", [P, D])
    rw = sb("rw", [E, D])
    rwT = sb("rwT", [P, KC, RN])
    ctx_sb = sb("ctx_sb", [S, B, D])
    ctxT = sb("ctxT", [P, KC, B, S])
    en = sb("en", [S, B, NF])
    esum = sb("esum", [S, B])
    ewide = sb("ewide", [S, B, P])
    ek = sb("ek", [P, B, S])
    emax = sb("emax", [P, B, 1])
    gate = sb("gate", [P, B, S])
    kT = sb("kT", [P, B, KC, S])
    k_hi = sb("k_hi", [P, B, KC, GS], f32r)
    k_lo = sb("k_lo", [P, B, KC, GS], f32r)
    vsb = sb("vsb", [S, B, D])
    vblock = sb("vblock", [CH, B, KC, 3, P])
    ident = sb("ident", [P, P])
    minus_half = sb("minus_half", [P, 1])
    xs = sb("xs", [P, 4, D])
    xb = sb("xb", [P, 4, D])
    st1, mv1, ve1, rs1 = sb("st1", [P, 6]), sb("mv1", [P, 4, 2]), sb("ve1", [P, 4, 1]), sb("rs1", [P, 4, 1])
    st2, mv2, ve2, rs2 = sb("st2", [P, 6]), sb("mv2", [P, 2, 2]), sb("ve2", [P, 2, 1]), sb("rs2", [P, 2, 1])
    xh = sb("xh", [P, 4, D])
    xT_hi = sb("xaT_hi", [P, 2, KC, 2 * P], f32r)
    xT_lo = sb("xaT_lo", [P, 2, KC, 2 * P], f32r)
    qT = sb("qT", [P, 2, 2 * P])
    q_hi = sb("q_hi", [P, 2, KC, 2 * P], f32r)
    q_lo = sb("q_lo", [P, 2, KC, 2 * P], f32r)
    probs = sb("probs", [P, 2, H, S])
    kblock = probs[:].rearrange("p b (m h) k -> p b m (h k)", m=KC)
    smax = sb("smax", [P, H])
    ssum = sb("ssum", [P, H])
    srec = sb("srec", [P, H])
    sinv = sb("sinv", [P, H])
    pT = sb("pT", [CH, 2, KC, 3, P])
    zeros = pT[:].rearrange("p j m q n -> p (j m q n)")[0:S, 0:KC * GS * P // S]
    o_hi = sb("o_hi", [P, 2, KC, P], f32r)
    o_lo = sb("o_lo", [P, 2, KC, P], f32r)
    late = sb("late", [P, 4, D])
    x2, x2h = late[:, 0:2, :], late[:, 2:4, :]
    wq = late[:]
    wo = wk[:]
    x2T = sb("x2T", [P, KC, P])

    ps_s = ctx.enter_context(nc.psum_tensor("ps_s", [P, KC, 512], f32))
    bank = [ctx.enter_context(nc.psum_tensor(f"bank{i}", [P, 512], f32)) for i in range(4, 8)]
    b4, b5, b6, b7 = bank

    ld_ctx, ld_wk, ld_wv, ld_wq, ld_wo = sem("ld_ctx"), sem("ld_wk"), sem("ld_wv"), sem("ld_wq"), sem("ld_wo")
    ld_small, ld_en = sem("ld_small"), sem("ld_en")
    consts_made, ident_made = sem("consts_made"), sem("ident_made")
    ctx_turned, ctxT_made = sem("ctx_turned"), sem("ctxT_made")
    energy_turned = sem("energy_turned")
    kv_product, v_made, gate_step, kblock_made = sem("kv_product"), sem("v_made"), sem("gate_step"), sem("kblock_made")
    zero_stored, v_stored, vblock_loaded, vblock_ready = sem("zero_stored"), sem("v_stored"), sem("vblock_loaded"), sem("vblock_ready")
    x_loaded = [sem(f"x_loaded{i}") for i in range(4)]
    st1_done, mv1_done, ve1_done, rs1_done, xh_done, xb_done = (
        sem("st1_done"), sem("mv1_done"), sem("ve1_done"), sem("rs1_done"), sem("xh_done"), sem("xb_done"))
    xh_turned, xT_hi_made, xT_lo_made = sem("xh_turned"), sem("xT_hi_made"), sem("xT_lo_made")
    wq_hi_made, wq_lo_made, q_product, qT_made = sem("wq_hi_made"), sem("wq_lo_made"), sem("q_product"), sem("qT_made")
    q_hi_made, q_lo_made, o_hi_made, o_lo_made = sem("q_hi_made"), sem("q_lo_made"), sem("o_hi_made"), sem("o_lo_made")
    k_hi_made, k_lo_made, wo_hi_made, wo_lo_made = sem("k_hi_made"), sem("k_lo_made"), sem("wo_hi_made"), sem("wo_lo_made")
    scores_done, max_done, shifted, exp_done = sem("scores_done"), sem("max_done"), sem("shifted"), sem("exp_done")
    sum_done, rec_done, inv_done, probs_done = sem("sum_done"), sem("rec_done"), sem("inv_done"), sem("probs_done")
    probs_turned, pT_made, av_product = sem("probs_turned"), sem("pT_made"), sem("av_product")
    o_product, x2_done, st2_done, mv2_done, ve2_done, rs2_done, x2h_done = (
        sem("o_product"), sem("x2_done"), sem("st2_done"), sem("mv2_done"), sem("ve2_done"), sem("rs2_done"), sem("x2h_done"))
    x2h_turned, x2T_made, logit_product, logits_copied = (
        sem("x2h_turned"), sem("x2T_made"), sem("logit_product"), sem("logits_copied"))
    x2_stored = [sem(f"x2_stored{i}") for i in range(2)]
    x2h_stored = [sem(f"x2h_stored{i}") for i in range(2)]

    x_v = x.rearrange("b (r p) d -> b r p d", p=P)
    out_v = out.rearrange("b (r p) d -> b r p d", p=P)
    xn2_v = xn2.rearrange("(b r p) d -> b r p d", b=B, p=P)
    SMALL = 16 * 5

    with nc.Block() as block:

        @block.sync
        def _(sp):
            def load_x(t):
                s = t.c % 4
                after(sp, xb_done, t.count(1, 1 - 4))
                sp.dma_start(xs[:, s, :], x_v[t.batch(), t.row()]).then_inc(x_loaded[s], 16)

            sp.dma_start(ctx_sb[:], context.rearrange("b s d -> s b d")).then_inc(ld_ctx, 16)
            sp.dma_start(wk[:], Wk.rearrange("(k p) n -> p k n", p=P)).then_inc(ld_wk, 16)
            for c in range(2):
                load_x(Tile(0, c))
            sp.dma_start(wq, Wq.rearrange("(k p) n -> p k n", p=P)).then_inc(ld_wq, 16)
            sp.dma_start(wv[:], Wv.rearrange("(k p) n -> p k n", p=P)).then_inc(ld_wv, 16)
            for c in range(2, 4):
                load_x(Tile(0, c))
            sp.wait_ge(kv_product, 2)
            sp.dma_start(wo, Wo.rearrange("(k p) n -> p k n", p=P)).then_inc(ld_wo, 16)
            sp.wait_ge(consts_made, 4)
            for b in range(B):
                sp.dma_start(vblocks[b].rearrange("m r c -> (m r) c").rearrange("(p q) c -> p (q c)", p=S),
                             zeros).then_inc(zero_stored, 16)
            sp.wait_ge(zero_stored, 32)
            for b in range(B):
                sp.wait_ge(v_made, b + 1)
                src = vsb[:, b, :].rearrange("k (m h d) -> k m h d", m=KC, h=HG)
                dst = vblocks[b].rearrange("m (h k) c -> k m h c", h=HG)
                for h in range(HG):
                    sp.dma_start(dst[:, :, h, h * DH:(h + 1) * DH], src[:, :, h, :]).then_inc(v_stored, 16)
                load_x(Tile(0, 4 + b))
            sp.wait_ge(v_stored, B * HG * 16)
            for b in range(B):
                for c in range(3):
                    r0 = 1 if c == 2 else 0
                    sp.dma_start(vblock[r0:CH, b, :, c, :],
                                 vblocks[b][:, CHUNK0[c] + r0:CHUNK0[c] + CH, :].rearrange("m r c -> r m c"))\
                      .then_inc(vblock_loaded, 16)

            def step(s):
                if s.c >= B and s.back(-4).exists():
                    load_x(s.back(-4))
                t = s.back(2)
                if t.exists():
                    j = t.c % 2
                    after(sp, x2_done, t.count(1, 1))
                    sp.dma_start(out_v[t.batch(), t.row()], x2[:, j, :]).then_inc(x2_stored[j], 16)
                    after(sp, x2h_done, t.count(1, 1))
                    sp.dma_start(xn2_v[t.batch(), t.row()], x2h[:, j, :]).then_inc(x2h_stored[j], 16)

            steps(sp, step)
            for j in range(2):
                sp.wait_ge(x2_stored[j], 16 * (TILES // 2))
                sp.wait_ge(x2h_stored[j], 16 * (TILES // 2))

        @block.gpsimd
        def _(pool):
            pool.memset(ident[:], 0.0).then_inc(ident_made, 1)
            pool.memset(minus_half[:], -0.5).then_inc(consts_made, 1)
            pool.memset(zeros, 0.0).then_inc(consts_made, 1)
            pool.memset(kblock, 0.0).then_inc(consts_made, 1)
            pool.memset(rwT[:], 0.0).then_inc(consts_made, 1)
            pool.wait_ge(ident_made, 1)
            pool.affine_select(out=ident[:], in_=ident[:], compare_op=ALU.not_equal, fill=1.0, base=0,
                               pattern=[[-1, P]], channel_multiplier=1).then_inc(ident_made, 1)
            pool.wait_ge(consts_made, 4)

            def normed(t):
                j = t.c % 4
                after(pool, xh_turned, t.count(1, -3))
                after(pool, ve1_done, t.count(1, 1))
                pool.tensor_tensor(rs1[:, j, :], ve1[:, j, :], minus_half[:], ALU.pow).then_inc(rs1_done, 1)
                after_apart(pool, rs1_done, t.count(1, 1), consts_made, 4)
                pool.tensor_scalar(xh[:, j, :], xs[:, t.c % 4, :], mv1[:, j, 0:1], rs1[:, j, :],
                                   ALU.subtract, ALU.mult).then_inc(xh_done, 1)

            def residual(t):
                after(pool, x2_done, t.count(1, -3))
                pool.tensor_tensor(xb[:, t.c % 4, :], xs[:, t.c % 4, :], bo_sb[:], ALU.add).then_inc(xb_done, 1)

            for c in range(4):
                normed(Tile(0, c))
            pool.wait_ge(ld_small, SMALL)

            def step(s):
                if s.back(-1).exists():
                    residual(s.back(-1))
                if s.c >= 0 and s.back(-4).exists():
                    normed(s.back(-4))
                t = s.back(2)
                if t.exists():
                    j = t.c % 2
                    after(pool, x2h_done, t.count(1, -1))
                    after(pool, ve2_done, t.count(1, 1))
                    pool.tensor_tensor(rs2[:, j, :], ve2[:, j, :], minus_half[:], ALU.pow).then_inc(rs2_done, 1)
                u = s.back(-2)
                if u.exists():
                    m = 2 * (u.c % 2)
                    after(pool, q_hi_made, u.count(1, 1))
                    pool.tensor_tensor(q_lo[:, u.pair(), m:m + 2], qT[:], q_hi[:, u.pair(), m:m + 2].bitcast(f32),
                                       ALU.subtract).then_inc(q_lo_made, 1)
                if s.c == 0 and isinstance(s.k, int):
                    pool.wait_ge(wo_hi_made, 1)
                    pool.tensor_tensor(wo_lo[:], wo, wo_hi[:].bitcast(f32), ALU.subtract).then_inc(wo_lo_made, 1)

            steps(pool, step)

        @block.scalar
        def _(act):
            act.dma_start(en[:], energy.rearrange("b s f -> s b f")).then_inc(ld_en, 16)
            with nc.allow_non_contiguous_dma(reason="biases, once"):
                act.dma_start(bq_sb[:], bq.rearrange("(m p) -> p m", p=P)).then_inc(ld_small, 16)
                act.dma_start(bk_sb[:], bk.rearrange("(m p) -> p m", p=P)).then_inc(ld_small, 16)
            act.dma_start(bv_sb[:], bv.partition_broadcast(S)).then_inc(ld_small, 16)
            act.dma_start(bo_sb[:], bo.partition_broadcast(P)).then_inc(ld_small, 16)
            act.dma_start(rw[:], router_w).then_inc(ld_small, 16)
            for b in range(B):
                act.wait_ge(ctx_turned, b + 1)
                act.activation(ctxT[:, :, b, :], bank[b][:, 0:KC * S].rearrange("p (k s) -> p k s", k=KC),
                               ACT.Copy).then_inc(ctxT_made, 1)
            act.wait_ge(ld_wq, 16)
            act.activation(wq_hi[:], wq, ACT.Copy).then_inc(wq_hi_made, 1)
            act.wait_ge(ctx_turned, 3)
            act.wait_ge(consts_made, 4)
            act.activation(rwT[:, :, 0:E], b6[:, 0:KC * E].rearrange("p (k e) -> p k e", k=KC),
                           ACT.Copy).then_inc(ctxT_made, 1)

            def step(s):
                t = s.back(-3)
                if t.exists():
                    h = t.c % 2
                    after(act, xh_turned, t.count(1, 1))
                    act.activation(xT_hi[:, t.pair(), :, h * P:(h + 1) * P],
                                   b4[:].rearrange("p (k n) -> p k n", k=KC), ACT.Copy).then_inc(xT_hi_made, 1)
                t = s.back(3)
                if t.exists():
                    after(act, x2h_turned, t.count(1, 1))
                    act.activation(x2T[:], b5[:].rearrange("p (k n) -> p k n", k=KC),
                                   ACT.Copy).then_inc(x2T_made, 1)
                    after(act, logit_product, t.count(1, 1))
                    act.activation(logits[:, t.batch(), t.row(), :], b4[:, 0:E], ACT.Copy).then_inc(logits_copied, 1)
                t = s.back(1)
                if t.exists():
                    if t.c == 0 and isinstance(t.k, int):
                        act.wait_ge(zero_stored, 32)
                    for q in range(3):
                        after(act, probs_turned, t.count(3, q + 1))
                        act.activation(pT[:, t.c % 2, :, q, :],
                                       [b6, b7, b4][q][0:CH, :].rearrange("p (m n) -> p m n", m=KC),
                                       ACT.Copy).then_inc(pT_made, 1)
                if s.exists():
                    after(act, shifted, s.count(1, 1))
                    act.activation(probs[:, s.c % 2], probs[:, s.c % 2], ACT.Exp).then_inc(exp_done, 1)
                u = s.back(-2)
                if u.exists():
                    m = 2 * (u.c % 2)
                    after(act, q_product, u.count(1, 1))
                    after(act, q_lo_made, u.count(1, 0))
                    for i in range(2):
                        act.activation(qT[:, i], b6[:, i * 2 * P:(i + 1) * 2 * P], ACT.Identity,
                                       bias=bq_sb[:, m + i:m + i + 1]).then_inc(qT_made, 1)
                    after(act, qT_made, u.count(2, 2))
                    act.activation(q_hi[:, u.pair(), m:m + 2], qT[:], ACT.Copy).then_inc(q_hi_made, 1)
                if s.c == FIRST + 1:
                    for b in range(B):
                        act.wait_ge(kblock_made, (b + 1) * HG)
                        act.activation(k_hi[:, b], kblock[:, b], ACT.Copy).then_inc(k_hi_made, 1)
                t = s.back(1)
                if t.exists():
                    after(act, av_product, t.count(1, 1))
                    act.activation(o_hi[:, t.c % 2], b7[:].rearrange("p (m n) -> p m n", m=KC),
                                   ACT.Copy).then_inc(o_hi_made, 1)
                if s.c == 0 and isinstance(s.k, int):
                    act.wait_ge(ld_wo, 16)
                    act.activation(wo_hi[:], wo, ACT.Copy).then_inc(wo_hi_made, 1)

            steps(act, step)

        @block.vector
        def _(dve):
            dve.memset(vblock[0:1, :, :, 2, :], 0.0).then_inc(vblock_ready, 1)
            dve.wait_ge(ld_en, 16)
            dve.tensor_reduce(esum[:], en[:], AX.X, ALU.add, apply_absolute_value=True).then_inc(gate_step, 1)
            dve.wait_ge(gate_step, 1)
            dve.tensor_scalar(ewide[:], esum[:].unsqueeze(2).to_broadcast([S, B, P]), 1.0 / NF, None,
                              ALU.mult).then_inc(gate_step, 1)
            dve.wait_ge(energy_turned, 1)
            energies = b7[:, 0:B * S].rearrange("p (b s) -> p b s", b=B)
            dve.tensor_reduce(emax[:], energies, AX.X, ALU.max).then_inc(gate_step, 1)
            dve.wait_ge(gate_step, 3)
            dve.tensor_scalar(emax[:], emax[:], 1e-8, None, ALU.add).then_inc(gate_step, 1)
            dve.wait_ge(gate_step, 4)
            dve.reciprocal(emax[:], emax[:]).then_inc(gate_step, 1)
            dve.wait_ge(gate_step, 5)
            dve.tensor_tensor(ek[:], energies, emax[:].to_broadcast([P, B, S]), ALU.mult).then_inc(gate_step, 1)
            dve.wait_ge(gate_step, 6)
            dve.tensor_scalar(gate[:], ek[:], THRESHOLD, 0.9, ALU.is_gt, ALU.mult).then_inc(gate_step, 1)
            dve.wait_ge(gate_step, 7)
            dve.tensor_scalar(gate[:], gate[:], 0.1, float(DH) ** -0.5, ALU.add, ALU.mult).then_inc(gate_step, 1)

            def stats(src, st, mv, ve, j, st_done, mv_done, ve_done, t):
                dve.bn_stats(st[:], src).then_inc(st_done, 1)
                after_apart(dve, st_done, t.count(1, 1), x_loaded[0], 16)
                dve.bn_aggr(mv[:, j, :], st[:]).then_inc(mv_done, 1)
                after(dve, mv_done, t.count(1, 1))
                dve.tensor_scalar(ve[:, j, :], mv[:, j, 1:2], ES, None, ALU.add).then_inc(ve_done, 1)

            def stats1(t):
                after(dve, x_loaded[t.c % 4], t.quarters(16, 16))
                after(dve, xh_done, t.count(1, -3))
                stats(xs[:, t.c % 4, :], st1, mv1, ve1, t.c % 4, st1_done, mv1_done, ve1_done, t)

            stats1(Tile(0, 0))
            stats1(Tile(0, 1))
            dve.wait_ge(ld_small, SMALL)
            dve.wait_ge(consts_made, 4)
            for j in range(2):
                dve.wait_ge(kv_product, j + 1)
                dve.tensor_tensor(kT[:, :, 2 * j:2 * j + 2, :],
                                  ps_s[:, j, 0:2 * B * S].rearrange("p (m b s) -> p b m s", m=2, b=B),
                                  bk_sb[:, 2 * j:2 * j + 2].unsqueeze(1).unsqueeze(3).to_broadcast([P, B, 2, S]),
                                  ALU.add).then_inc(gate_step, 1)
            dve.wait_ge(wq_hi_made, 1)
            dve.tensor_tensor(wq_lo[:], wq, wq_hi[:].bitcast(f32), ALU.subtract).then_inc(wq_lo_made, 1)

            def key_blocks():
                dve.wait_ge(gate_step, 10)
                for b in range(B):
                    for h in range(HG):
                        r = slice(h * DH, (h + 1) * DH)
                        dve.tensor_tensor(kblock[r, b, :, h * S:(h + 1) * S], kT[r, b],
                                          gate[r, b, :].unsqueeze(1).to_broadcast([DH, KC, S]),
                                          ALU.mult).then_inc(kblock_made, 1)

            def values(b):
                dve.wait_ge(kv_product, 3 + b)
                dve.tensor_tensor(vsb[:, b, :], ps_s[0:S, 2 + b, :], bv_sb[:], ALU.add).then_inc(v_made, 1)

            def step(s):
                t = s.back(-3)
                if t.exists():
                    h = t.c % 2
                    part = xT_hi[:, t.pair(), :, h * P:(h + 1) * P]
                    after(dve, xT_hi_made, t.count(1, 1))
                    dve.tensor_tensor(xT_lo[:, t.pair(), :, h * P:(h + 1) * P],
                                      b4[:].rearrange("p (k n) -> p k n", k=KC), part.bitcast(f32),
                                      ALU.subtract).then_inc(xT_lo_made, 1)
                if s.c == FIRST + 1:
                    for c in range(2, 4):
                        stats1(Tile(0, c))
                    key_blocks()
                    values(0)
                if s.c == FIRST + 2:
                    for b in range(B):
                        dve.wait_ge(k_hi_made, b + 1)
                        dve.tensor_tensor(k_lo[:, b], kblock[:, b], k_hi[:, b].bitcast(f32), ALU.subtract)\
                           .then_inc(k_lo_made, 1)
                    values(1)
                if s.c in (0, 1):
                    stats1(s.back(-4))
                if s.exists():
                    sc = ps_s[:, :, 0:GS].rearrange("p m (h k) -> p m h k", h=HG)
                    after(dve, scores_done, s.count(1, 1))
                    dve.tensor_reduce(smax[:].rearrange("p (m h) -> p m h", m=KC), sc, AX.X,
                                      ALU.max).then_inc(max_done, 1)
                    after(dve, max_done, s.count(1, 1))
                    dve.tensor_tensor(probs[:, s.c % 2].rearrange("p (m h) k -> p m h k", m=KC), sc,
                                      smax[:].rearrange("p (m h) -> p m h", m=KC).unsqueeze(3)
                                      .to_broadcast([P, KC, HG, S]), ALU.subtract).then_inc(shifted, 1)
                if s.c > 1 and s.back(-4).exists():
                    stats1(s.back(-4))
                t = s.back(2)
                if t.exists():
                    j = t.c % 2
                    after(dve, o_product, t.count(1, 1))
                    after(dve, xb_done, t.count(1, 1))
                    after(dve, x2_stored[j], t.halves(16, 0))
                    after(dve, x2h_done, t.count(1, -1))
                    dve.tensor_tensor(x2[:, j, :], b5[:], xb[:, t.c % 4, :], ALU.add).then_inc(x2_done, 1)
                    after(dve, x2_done, t.count(1, 1))
                    stats(x2[:, j, :], st2, mv2, ve2, j, st2_done, mv2_done, ve2_done, t)
                if s.exists():
                    after(dve, exp_done, s.count(1, 1))
                    dve.tensor_reduce(ssum[:], probs[:, s.c % 2], AX.X, ALU.add).then_inc(sum_done, 1)
                    after(dve, sum_done, s.count(1, 1))
                    dve.reciprocal(srec[:], ssum[:]).then_inc(rec_done, 1)
                    after(dve, rec_done, s.count(1, 1))
                    dve.tensor_scalar(sinv[:], srec[:], 0.0, None, ALU.max).then_inc(inv_done, 1)
                t = s.back(2)
                if t.exists():
                    j = t.c % 2
                    after(dve, x2h_stored[j], t.halves(16, 0))
                    after_apart(dve, rs2_done, t.count(1, 1), x_loaded[0], 16)
                    dve.tensor_scalar(x2h[:, j, :], x2[:, j, :], mv2[:, j, 0:1], rs2[:, j, :],
                                      ALU.subtract, ALU.mult).then_inc(x2h_done, 1)
                if s.exists():
                    after(dve, inv_done, s.count(1, 1))
                    dve.scalar_tensor_tensor(probs[:, s.c % 2], probs[:, s.c % 2], 0.0,
                                             sinv[:].unsqueeze(2).to_broadcast([P, H, S]),
                                             ALU.max, ALU.mult).then_inc(probs_done, 1)
                t = s.back(1)
                if t.exists():
                    after(dve, o_hi_made, t.count(1, 1))
                    dve.tensor_tensor(o_lo[:, t.c % 2], b7[:].rearrange("p (m n) -> p m n", m=KC),
                                      o_hi[:, t.c % 2].bitcast(f32), ALU.subtract).then_inc(o_lo_made, 1)

            steps(dve, step)

        @block.tensor
        def _(pe):
            pe.wait_ge(ident_made, 2)
            pe.wait_ge(ld_ctx, 16)
            for b in range(B):
                for k in range(KC):
                    last = pe.transpose(bank[b][:, k * S:(k + 1) * S], ctx_sb[:, b, k * P:(k + 1) * P],
                                        ident[0:S, 0:S])
                last.then_inc(ctx_turned, 1)
            pe.wait_ge(gate_step, 2)
            for b in range(B):
                last = pe.transpose(b7[:, b * S:(b + 1) * S], ewide[:, b, :], ident[0:S, 0:S])
            last.then_inc(energy_turned, 1)
            pe.wait_ge(ld_wk, 16)
            pe.wait_ge(ctxT_made, 2)
            for m in range(KC):
                for k in range(KC):
                    last = pe.matmul(ps_s[:, m // 2, m % 2 * B * S:(m % 2 + 1) * B * S], wk[:, k, m * P:(m + 1) * P],
                                     ctxT[:, k].rearrange("p b s -> p (b s)"), start=(k == 0), stop=(k == KC - 1))
                if m % 2:
                    last.then_inc(kv_product, 1)
            pe.wait_ge(ld_small, SMALL)
            for k in range(KC):
                last = pe.transpose(b6[:, k * E:(k + 1) * E], rw[:, k * P:(k + 1) * P], ident[0:E, 0:E])
            last.then_inc(ctx_turned, 1)
            pe.wait_ge(ctxT_made, 3)

            def values(b):
                pe.wait_ge(ld_wv, 16)
                for k in range(KC):
                    last = pe.matmul(ps_s[0:S, 2 + b, :], ctxT[:, k, b, :], wv[:, k, :],
                                     start=(k == 0), stop=(k == KC - 1))
                last.then_inc(kv_product, 1)

            def step(s):
                t = s.back(-3)
                if t.exists():
                    after(pe, xh_done, t.count(1, 1))
                    after(pe, xT_lo_made, t.count(1, 0))
                    after(pe, pT_made, s.back(2).count(3, 3))
                    after(pe, logits_copied, s.back(4).count(1, 1))
                    for k in range(KC):
                        last = pe.transpose(b4[:, k * P:(k + 1) * P], xh[:, t.c % 4, k * P:(k + 1) * P], ident[:])
                    last.then_inc(xh_turned, 1)
                t = s.back(3)
                if t.exists():
                    after(pe, x2h_done, t.count(1, 1))
                    for k in range(KC):
                        last = pe.transpose(b5[:, k * P:(k + 1) * P], x2h[:, t.c % 2, k * P:(k + 1) * P], ident[:])
                    last.then_inc(x2h_turned, 1)
                if s.exists():
                    if s.c == 0 and isinstance(s.k, int):
                        pe.wait_ge(v_made, B)
                    if s.c < B and isinstance(s.k, int):
                        pe.wait_ge(k_lo_made, s.c + 1)
                    if s.c % 2 == 0:
                        after(pe, q_lo_made, s.count(1, 2))
                    after(pe, shifted, s.count(1, 0))
                    j, b, tokens = s.pair(), s.batch(), slice(s.c % 2 * P, (s.c % 2 + 1) * P)
                    for m in range(KC):
                        for i, (q, k) in enumerate(PARTS):
                            last = pe.matmul(ps_s[:, m, 0:GS], (q_hi, q_lo)[q][:, j, m, tokens],
                                             (k_hi, k_lo)[k][:, b, m, :], start=(i == 0), stop=(i == 2))
                    last.then_inc(scores_done, 1)
                t = s.back(3)
                if t.exists():
                    after(pe, x2T_made, t.count(1, 1))
                    after(pe, xT_lo_made, min_tile(s.back(-3), 1))
                    for k in range(KC):
                        last = pe.matmul(b4[:, 0:RN], x2T[:, k, :], rwT[:, k, :], start=(k == 0), stop=(k == KC - 1))
                    last.then_inc(logit_product, 1)
                t = s.back(1)
                if t.exists():
                    j = t.c % 2
                    after(pe, probs_done, t.count(1, 1))
                    flat = probs[:, j].rearrange("p h k -> p (h k)")
                    for q in range(3):
                        if q == 0:
                            after(pe, qT_made, min_tile(s.back(-1), 2))
                        if q == 1:
                            after(pe, o_lo_made, t.count(1, 0))
                        if q == 2:
                            after(pe, xT_lo_made, min_tile(s.back(-3), 1))
                            after(pe, logits_copied, s.back(3).count(1, 1))
                        for m in range(KC):
                            c0 = m * GS + CHUNK0[q]
                            last = pe.transpose([b6, b7, b4][q][0:CH, m * P:(m + 1) * P],
                                                flat[:, c0:c0 + CH], ident[:])
                        last.then_inc(probs_turned, 1)
                t = s.back(2)
                if t.exists():
                    if t.c == 0 and isinstance(t.k, int):
                        pe.wait_ge(wo_lo_made, 1)
                    j = t.c % 2
                    after(pe, o_lo_made, t.count(1, 1))
                    if s.back(3).exists():
                        after(pe, x2T_made, s.back(3).count(1, 1))
                    for m in range(KC):
                        for i, (a, w) in enumerate(PARTS):
                            last = pe.matmul(b5[:], (o_hi, o_lo)[a][:, j, m, :], (wo_hi, wo_lo)[w][:, m, :],
                                             start=(m == 0 and i == 0), stop=(m == KC - 1 and i == 2))
                    last.then_inc(o_product, 1)
                u = s.back(-2)
                if u.exists():
                    m0 = 2 * (u.c % 2)
                    if u.c == 0 and isinstance(u.k, int):
                        pe.wait_ge(wq_lo_made, 1)
                    if u.c % 2 == 0:
                        after(pe, xT_lo_made, u.count(1, 2))
                    after(pe, qT_made, u.count(2, 0))
                    if s.back(1).exists():
                        after(pe, pT_made, s.back(1).count(3, 1))
                    for m in range(2):
                        cols = slice((m0 + m) * P, (m0 + m + 1) * P)
                        for i, (w, a) in enumerate(PARTS):
                            for k in range(KC):
                                last = pe.matmul(b6[:, m * 2 * P:(m + 1) * 2 * P], (wq_hi, wq_lo)[w][:, k, cols],
                                                 (xT_hi, xT_lo)[a][:, u.pair(), k, :],
                                                 start=(i == 0 and k == 0), stop=(i == 2 and k == KC - 1))
                    last.then_inc(q_product, 1)
                    if u.c < B and isinstance(u.k, int):
                        values(u.c)
                t = s.back(1)
                if t.exists():
                    j, b = t.c % 2, t.batch()
                    if t.c == 0 and isinstance(t.k, int):
                        pe.wait_ge(vblock_ready, 1)
                        pe.wait_ge(vblock_loaded, B * 3 * 16)
                    after(pe, pT_made, t.count(3, 3))
                    for m in range(KC):
                        for q in range(3):
                            last = pe.matmul(b7[:, m * P:(m + 1) * P], vblock[:, b, m, q, :], pT[:, j, m, q, :],
                                             start=(q == 0), stop=(q == 2))
                    last.then_inc(av_product, 1)

            def min_tile(t, per):
                return t.count(per, per) if t.exists() else TILES * per

            steps(pe, step)


def experts(nc, ctx, logits, wg, wu, wd, out, xn2):

    def sb(name, shape, dt=f32):
        return ctx.enter_context(nc.sbuf_tensor(name, shape, dt))

    def sem(name):
        return ctx.enter_context(nc.semaphore(name))

    lt = logits[:].rearrange("p b r e -> p (b r) e")
    T32 = TILES
    pr = sb("pr", [P, T32, E])
    wa = sb("wa", [P, T32, E])
    wb = sb("wb", [P, T32, E])
    oh1 = sb("oh1", [P, T32, E])
    oh2 = sb("oh2", [P, T32, E])
    r1, r2, r3, r4 = (sb(f"r{i}", [P, T32]) for i in range(1, 5))
    rev = sb("rev", [P, E])
    ident = sb("ident2", [P, P])
    same = sb("same", [P, P])
    before = sb("before", [P, P])
    wt = sb("wt", [P, 2, E, SEG])
    key = sb("key", [P, 2 * P])
    gt, eq, eqv, scan, keep, posm = (sb(n, [P, 2 * P]) for n in ("gt", "eq", "eqv", "scan", "keep", "posm"))
    zrow = sb("zrow", [P, 2 * P])
    thr, unit, pick = (sb(n, [P, 1], i32) for n in ("thr", "unit", "pick"))
    cand, digits, picks = (sb(n, [P, 3], i32) for n in ("cand", "digits", "picks"))
    cnt3 = sb("cnt3", [P, 3], bf16)
    key_high = sb("key_high", [P, 2 * P], bf16)
    above_high = sb("above_high", [P, 3, 2 * P], bf16)
    same_b = sb("same_b", [P, P], bf16)
    posi = sb("posi", [P, E, SEG, 2], i32)
    pick_f, cgt, ceq, off, ned, ckp = (sb(n, [P, 1]) for n in ("pick_f", "cgt", "ceq", "off", "ned", "ckp"))
    pos = sb("pos", [P, 2, E, SEG])
    hi_ = sb("hi_", [P, E, SEG, 2], i32)
    lo_ = sb("lo_", [P, E, SEG, 2], i32)
    rem = sb("rem", [P, E, SEG, 2])
    rem2 = sb("rem2", [P, E, SEG, 2])
    vals = sb("vals", [P, E, T32, NV], bf16)
    iota_p = sb("iota_p", [P, P], i32)
    iota_c = sb("iota_c", [P, CT], i32)
    hot = sb("hot", [P, T32, P], bf16)
    jhot = sb("jhot", [P, T32, CT], bf16)
    vhot = sb("vhot", [P, T32, CT, NV], bf16)
    lst = sb("lst", [P, CT, NV])
    lid = sb("lid", [P, CT])
    lid2 = sb("lid2", [P, CT])
    lw = sb("lw", [P, CT])
    gidx = sb("gidx", [P, CT], i32)
    sidx_next, sidx = sb("sidx_next", [P, CT], i32), sb("sidx", [P, CT], i32)
    wslot_next, wslot = sb("wslot_next", [P, CT]), sb("wslot", [P, CT])
    xg = sb("xg", [P, CT, D])
    xT_hi = sb("xT_hi", [P, KC, CAP], f32r)
    xT_lo = sb("xT_lo", [P, KC, CAP], f32r)
    raw_gu = sb("raw_gu", [P, 2, 2, KC, 2 * P])
    raw_d = sb("raw_d", [P, 2, 2, D])
    gu_hi = sb("gu_hi", [P, 2, 2, KC, P], f32r)
    gu_lo = sb("gu_lo", [P, 2, 2, KC, P], f32r)
    d_hi = sb("d_hi", [P, 2, D], f32r)
    d_lo = sb("d_lo", [P, 2, D], f32r)
    sil = sb("sil", [P, CAP])
    hid = sb("hid", [P, CAP])
    h_hi = sb("h_hi", [P, 2, CAP], f32r)
    h_lo = sb("h_lo", [P, 2, CAP], f32r)
    ys = sb("ys", [P, CT, D])

    y = [ctx.enter_context(nc.psum_tensor(f"y{i}", [P, D], f32)) for i in range(CT)]
    ga = ctx.enter_context(nc.psum_tensor("ga", [P, 512], f32))
    gb = ctx.enter_context(nc.psum_tensor("gb", [P, 512], f32))
    ub = ctx.enter_context(nc.psum_tensor("ub", [P, 512], f32))

    consts, rev_made, high_made = sem("consts"), sem("rev_made"), sem("high_made")
    chain = sem("chain")
    shift_done, probs_exp = sem("shift_done"), sem("probs_exp")
    wt_done, wt_turned, key_done = sem("wt_done"), sem("wt_turned"), sem("key_done")
    counted, totalled, cand_done, picked, thr_done, unit_done = (
        sem("counted"), sem("totalled"), sem("cand_done"), sem("picked"), sem("thr_done"), sem("unit_done"))
    reached, digits_made, digits_done, split_step, values_done = (
        sem("reached"), sem("digits_made"), sem("digits_done"), sem("split_step"), sem("values_done"))
    tallied, tally_sum, kept, kept_sum, posm_done, pos_turned = (
        sem("tallied"), sem("tally_sum"), sem("kept"), sem("kept_sum"), sem("posm_done"), sem("pos_turned"))
    slots_done = sem("slots_done")
    hot_done, jhot_done, vhot_done, list_product, list_read, list_made = (
        sem("hot_done"), sem("jhot_done"), sem("vhot_done"), sem("list_product"), sem("list_read"), sem("list_made"))
    list_step, slots_listed = sem("list_step"), sem("slots_listed")
    gathered, xg_turned, xT_hi_done, xT_lo_done = (
        [sem(f"gathered{t}") for t in range(CT)], sem("xg_turned"), sem("xT_hi_done"), sem("xT_lo_done"))
    gu_loaded = [sem(f"gu_loaded{i}") for i in range(2)]
    d_loaded = [sem(f"d_loaded{i}") for i in range(2)]
    gu_hi_done, gu_lo_done, d_hi_done, d_lo_done = (
        sem("gu_hi_done"), sem("gu_lo_done"), sem("d_hi_done"), sem("d_lo_done"))
    a_product, gb_product, ub_product, y_product, y_finished = (
        sem("a_product"), sem("gb_product"), sem("ub_product"), sem("y_product"),
        sem("y_finished"))
    sil_done, hid_done, h_hi_done, h_lo_done = sem("sil_done"), sem("hid_done"), sem("h_hi_done"), sem("h_lo_done")
    ys_act, ys_dve, scattered, slots_moved = sem("ys_act"), sem("ys_dve"), sem("scattered"), sem("slots_moved")

    wg_v = wg.rearrange("e (k p) (q f) -> e q p k f", p=P, f=2 * P)
    wu_v = wu.rearrange("e (k p) (q f) -> e q p k f", p=P, f=2 * P)
    wd_v = wd.rearrange("e (q c p) d -> e q p c d", p=P, c=2)
    out_rows = out.rearrange("b l d -> (b l) d")
    PAIRS = FC // 2

    def make_values(eng, e):
        after(eng, list_product, e)
        eng.tensor_tensor(jhot[:], iota_c[:].unsqueeze(1).to_broadcast([P, T32, CT]),
                          hi_[:, e].rearrange("p s two -> p (s two)").unsqueeze(2).to_broadcast([P, T32, CT]),
                          ALU.is_equal).then_inc(jhot_done, 1)
        after(eng, jhot_done, e + 1)
        eng.tensor_tensor(vhot[:], jhot[:].unsqueeze(3).to_broadcast([P, T32, CT, NV]),
                          vals[:, e].unsqueeze(2).to_broadcast([P, T32, CT, NV]),
                          ALU.mult).then_inc(vhot_done, 1)

    def make_hots(eng, e, piece):
        place = lo_[:, e].rearrange("p s two -> p (s two)")[:, bass.ds(piece * HOT, HOT)]
        eng.tensor_tensor(hot[:, bass.ds(piece * HOT, HOT), :], iota_p[:].unsqueeze(1).to_broadcast([P, HOT, P]),
                          place.unsqueeze(2).to_broadcast([P, HOT, P]), ALU.is_equal).then_inc(hot_done, 1)

    class Chunk:

        def __init__(self, e, k, c):
            self.e, self.k, self.c = e, k, c

        def count(self, per, extra):
            return self.e * (FC * per) + self.k * (4 * per) + (self.c * per + extra)

        def pairs(self, per, extra):
            return self.e * (FC // 4 * per) + self.k * per + ((self.c // 4) * per + extra)

        def ahead(self, n):
            return Chunk(self.e, self.k, self.c + n)

        def exists(self):
            return not isinstance(self.e, int) or self.e * FC + self.c < E * FC

    def run_chunks(eng, e, chunk):
        chunk(Chunk(e, 0, 0))
        chunk(Chunk(e, 0, 1))
        with eng.Fori(0, (FC - 4) // 4) as k:
            for c in range(2, 6):
                chunk(Chunk(e, k, c))
        chunk(Chunk(e, 0, FC - 2))
        chunk(Chunk(e, 0, FC - 1))

    def run_experts(eng, expert):
        expert(0, True)
        with eng.Fori(1, E - 1) as e:
            expert(e, True)
        expert(E - 1, False)

    with nc.Block() as block:

        @block.sync
        def _(sp):
            def load(e, q, slot, uses):
                after(sp, gu_hi_done, uses(2, 0))
                after(sp, gu_lo_done, uses(2, 0))
                sp.dma_start(raw_gu[:, slot, 0], wg_v[e, q]).then_inc(gu_loaded[slot], 16)
                sp.dma_start(raw_gu[:, slot, 1], wu_v[e, q]).then_inc(gu_loaded[slot], 16)
                after(sp, d_hi_done, uses(2, 0))
                after(sp, d_lo_done, uses(2, 0))
                sp.dma_start(raw_d[:, slot], wd_v[e, q]).then_inc(d_loaded[slot], 16)

            for q in range(2):
                load(0, q, q, lambda per, extra: 0)
            with sp.Fori(0, (PAIRS - 2) // 2) as k:
                for j in range(2):
                    load(0, k * 2 + (2 + j), j, lambda per, extra, j=j: k * 4 + (2 * (2 + j) - 2))
            with sp.Fori(1, E) as e:
                with sp.Fori(0, PAIRS // 2) as k:
                    for j in range(2):
                        load(e, k * 2 + j, j, lambda per, extra, j=j: e * FC + k * 4 + (2 * j - 2))

        @block.gpsimd
        def _(pool):
            pool.iota(rev[:], [[-1, E]], base=E, channel_multiplier=0,
                      allow_small_or_imprecise_dtypes=True).then_inc(rev_made, 1)
            pool.memset(ident[:], 0.0).then_inc(consts, 1)
            pool.memset(same[:], 1.0).then_inc(consts, 1)
            pool.memset(zrow[:], 0.0).then_inc(consts, 1)
            pool.memset(thr[:], 0).then_inc(consts, 1)
            for j in range(3):
                pool.memset(digits[:, j:j + 1], (j + 1) << (BITS - 2)).then_inc(digits_made, 1)
            pool.memset(unit[:], 1 << (BITS - 2)).then_inc(consts, 1)
            pool.iota(iota_p[:], [[1, P]], base=0, channel_multiplier=0,
                      allow_small_or_imprecise_dtypes=True).then_inc(consts, 1)
            pool.iota(iota_c[:], [[1, CT]], base=0, channel_multiplier=0,
                      allow_small_or_imprecise_dtypes=True).then_inc(consts, 1)
            pool.iota(vals[:, :, :, 0], [[0, E], [1, T32]], base=0, channel_multiplier=0,
                      allow_small_or_imprecise_dtypes=True).then_inc(consts, 1)
            pool.iota(vals[:, :, :, 1], [[0, E], [0, T32]], base=0, channel_multiplier=1,
                      allow_small_or_imprecise_dtypes=True).then_inc(consts, 1)
            pool.memset(vals[:, :, :, 2], 1.0).then_inc(consts, 1)
            pool.wait_ge(consts, 10)
            pool.affine_select(out=ident[:], in_=ident[:], compare_op=ALU.not_equal, fill=1.0, base=0,
                               pattern=[[-1, P]], channel_multiplier=1).then_inc(consts, 1)
            pool.affine_select(out=same[:], in_=same[:], compare_op=ALU.is_ge, fill=0.0, base=0,
                               pattern=[[-SEG, E], [0, SEG]], channel_multiplier=1).then_inc(consts, 1)
            pool.wait_ge(consts, 12)
            pool.affine_select(out=same[:], in_=same[:], compare_op=ALU.is_ge, fill=0.0, base=SEG - 1,
                               pattern=[[SEG, E], [0, SEG]], channel_multiplier=-1).then_inc(consts, 1)
            pool.wait_ge(consts, 13)
            pool.tensor_copy(same_b[:], same[:]).then_inc(consts, 1)
            pool.affine_select(out=before[:], in_=same[:], compare_op=ALU.is_gt, fill=0.0, base=0,
                               pattern=[[1, P]], channel_multiplier=-1).then_inc(consts, 1)

            def scatter(e):
                after(pool, scattered, e * (16 * CT))
                for t in range(CT):
                    if t < 3:
                        after_apart(pool, ys_act, e * 3 + (t + 1), consts, 15)
                    else:
                        after_apart(pool, ys_dve, e * 2 + (t - 2), consts, 15)
                    pool.indirect_dma_start(
                        out=out_rows, out_offset=bass.IndirectOffsetOnAxis(ap=sidx[:, t:t + 1], axis=0),
                        in_=ys[:, t, :], in_offset=None, bounds_check=N - 1, oob_is_err=False,
                        compute_op=ALU.add).then_inc(scattered, 16)

            def gather(e):
                after(pool, list_made, e + 1)
                after_apart(pool, xg_turned, e * CT, consts, 15)
                for t in range(CT):
                    pool.indirect_dma_start(
                        out=xg[:, t, :], out_offset=None, in_=xn2,
                        in_offset=bass.IndirectOffsetOnAxis(ap=gidx[:, t:t + 1], axis=0),
                        bounds_check=N - 1, oob_is_err=False).then_inc(gathered[t], 16)

            pool.wait_ge(wt_done, 1)
            weights = wt[:].rearrange("p two e s -> p e s two")
            parts = vals[:].rearrange("p e (s two) v -> p e s two v", two=2)
            pool.tensor_copy(parts[:, :, :, :, 3], weights).then_inc(split_step, 1)
            pool.wait_ge(split_step, 1)
            pool.tensor_tensor(rem[:], weights, parts[:, :, :, :, 3], ALU.subtract).then_inc(split_step, 1)
            pool.wait_ge(split_step, 2)
            pool.tensor_copy(parts[:, :, :, :, 4], rem[:]).then_inc(split_step, 1)
            pool.wait_ge(split_step, 3)
            pool.tensor_tensor(rem2[:], rem[:], parts[:, :, :, :, 4], ALU.subtract).then_inc(split_step, 1)
            pool.wait_ge(split_step, 4)
            pool.tensor_copy(parts[:, :, :, :, 5], rem2[:]).then_inc(values_done, 1)
            gather(0)

            def expert(e, more):
                if more:
                    gather(e + 1)
                scatter(e)

            run_experts(pool, expert)
            pool.wait_ge(scattered, 16 * CT * E)

        @block.scalar
        def _(act):
            act.wait_ge(shift_done, 1)
            act.activation(pr[:], pr[:], ACT.Exp).then_inc(probs_exp, 1)

            def split_gu(c):
                if not c.exists():
                    return
                s, pair = c.c % 2, c.c // 2 % 2
                after(act, gu_loaded[pair], c.pairs(32, 32))
                after(act, ub_product, c.count(1, -1))
                act.activation(gu_hi[:, s], raw_gu[:, pair, :, :, s * P:(s + 1) * P],
                               ACT.Copy).then_inc(gu_hi_done, 1)

            def split_d(c):
                if not c.exists():
                    return
                s, pair = c.c % 2, c.c // 2 % 2
                after(act, d_loaded[pair], c.pairs(16, 16))
                after(act, y_product, c.count(1, -1))
                act.activation(d_hi[:, s], raw_d[:, pair, s, :], ACT.Copy).then_inc(d_hi_done, 1)

            def turned(e, tiles):
                for t in tiles:
                    after(act, xg_turned, e * CT + (t + 1))
                    act.activation(xT_hi[:, :, t * P:(t + 1) * P],
                                   [ga, gb, ub][t % 3][:].rearrange("p (k n) -> p k n", k=KC),
                                   ACT.Copy).then_inc(xT_hi_done, 1)

            split_gu(Chunk(0, 0, 0))
            split_gu(Chunk(0, 0, 1))
            split_d(Chunk(0, 0, 0))
            turned(0, range(CT))

            def expert(e, more):
                def chunk(c):
                    s = c.c % 2
                    after(act, a_product, c.count(1, 1))
                    after(act, hid_done, c.count(2, 0))
                    act.activation(sil[:, 0:NA], ga[:, 0:NA], ACT.Silu).then_inc(sil_done, 1)
                    after(act, gb_product, c.count(1, 1))
                    act.activation(sil[:, NA:CAP], gb[:, 0:NB], ACT.Silu).then_inc(sil_done, 1)
                    if c.c == FC - 1 and more:
                        turned(e + 1, range(1))
                    split_gu(c.ahead(2))
                    after(act, hid_done, c.count(2, 2))
                    act.activation(h_hi[:, s, :], hid[:], ACT.Copy).then_inc(h_hi_done, 1)
                    split_d(c.ahead(1))

                run_chunks(act, e, chunk)
                if more:
                    turned(e + 1, range(1, CT))
                after(act, slots_moved, e * 2 + 2)
                after(act, scattered, e * (16 * CT))
                for t in range(3):
                    after(act, y_finished, e * (CT - 1) + (t + 1))
                    act.activation(ys[:, t, :], y[t][:], ACT.Copy, scale=wslot[:, t:t + 1]).then_inc(ys_act, 1)

            run_experts(act, expert)

        @block.vector
        def _(dve):
            n = [0]

            def link(ins):
                n[0] += 1
                ins.then_inc(chain, 1)
                dve.wait_ge(chain, n[0])

            def over_e(a):
                return a[:].unsqueeze(2).to_broadcast([P, T32, E])

            link(dve.tensor_reduce(r1[:], lt, AX.X, ALU.max))
            dve.tensor_tensor(pr[:], lt, over_e(r1), ALU.subtract).then_inc(shift_done, 1)
            dve.wait_ge(probs_exp, 1)
            link(dve.tensor_reduce(r2[:], pr[:], AX.X, ALU.add))
            link(dve.reciprocal(r3[:], r2[:]))
            link(dve.tensor_tensor(pr[:], pr[:], over_e(r3), ALU.mult))
            dve.wait_ge(rev_made, 1)
            rev_b = rev[:].unsqueeze(1).to_broadcast([P, T32, E])

            def first_max(src, top, one_hot):
                link(dve.tensor_reduce(top[:], src[:], AX.X, ALU.max))
                link(dve.tensor_tensor(wa[:], src[:], over_e(top), ALU.is_equal))
                link(dve.tensor_tensor(wa[:], wa[:], rev_b, ALU.mult))
                link(dve.tensor_reduce(r4[:], wa[:], AX.X, ALU.max))
                link(dve.tensor_tensor(one_hot[:], wa[:], over_e(r4), ALU.is_equal))

            first_max(pr, r1, oh1)
            link(dve.scalar_tensor_tensor(wb[:], oh1[:], -2.0, pr[:], ALU.mult, ALU.add))
            first_max(wb, r2, oh2)
            link(dve.tensor_tensor(r3[:], r1[:], r2[:], ALU.add))
            link(dve.tensor_scalar(r3[:], r3[:], 1e-6, None, ALU.add))
            link(dve.reciprocal(r3[:], r3[:]))
            dve.tensor_tensor(wa[:], pr[:], over_e(r3), ALU.mult).then_inc(chain, 1)
            n[0] += 1
            link(dve.tensor_tensor(wb[:], oh1[:], oh2[:], ALU.add))
            sep = "p (s two) e -> p s two e"
            dve.tensor_tensor(wt[:].rearrange("p two e s -> p s two e"), wa[:].rearrange(sep, two=2),
                              wb[:].rearrange(sep, two=2), ALU.mult).then_inc(wt_done, 1)
            dve.wait_ge(wt_turned, 1)
            dve.tensor_copy(key[:], ga[:, 0:2 * P]).then_inc(key_done, 1)
            dve.wait_ge(key_done, 1)

            dve.wait_ge(digits_made, 3)
            dve.wait_ge(consts, 15)
            dve.tensor_copy(key_high[:], key[:].bitcast(bf16)[:, 1::2]).then_inc(high_made, 1)
            dve.wait_ge(high_made, 1)

            def find_digit(done, keys, above):
                dve.tensor_tensor(cand[:], thr[:].to_broadcast([P, 3]), digits[:], ALU.bitwise_or)\
                   .then_inc(cand_done, 1)
                dve.wait_ge(cand_done, done)
                for j in range(3):
                    dve.tensor_scalar(above[j], keys[:], cand[:, j:j + 1].bitcast(f32), 0.0, ALU.is_ge, ALU.add,
                                      accum_out=cnt3[:, j:j + 1]).then_inc(counted, 1)
                after(dve, unit_done, done - 1)
                dve.tensor_scalar(digits[:], digits[:], 2, None, ALU.logical_shift_right).then_inc(digits_done, 1)
                dve.wait_ge(totalled, done)
                dve.scalar_tensor_tensor(picks[:], gb[:, 0:3], float(CAP), unit[:].to_broadcast([P, 3]),
                                         ALU.is_ge, ALU.mult, accum_out=pick_f[:]).then_inc(reached, 1)
                dve.wait_ge(reached, done)
                dve.tensor_copy(pick[:], pick_f[:]).then_inc(picked, 1)
                dve.wait_ge(picked, done)
                dve.tensor_tensor(thr[:], thr[:], pick[:], ALU.bitwise_or).then_inc(thr_done, 1)
                dve.wait_ge(digits_done, done)
                dve.tensor_scalar(unit[:], unit[:], 2, None, ALU.logical_shift_right).then_inc(unit_done, 1)
                dve.wait_ge(thr_done, done)

            for u in range(HIGH):
                find_digit(u + 1, key_high, [above_high[:, j] for j in range(3)])
            with dve.Fori(0, (PAIRS_OF_BITS - HIGH) // SEARCH) as turn:
                for u in range(SEARCH):
                    find_digit(turn * SEARCH + (HIGH + u + 1), key, (eq[:], eqv[:], scan[:]))

            def split_gu(c):
                if not c.exists():
                    return
                s, pair = c.c % 2, c.c // 2 % 2
                after(dve, gu_hi_done, c.count(1, 1))
                dve.tensor_tensor(gu_lo[:, s], raw_gu[:, pair, :, :, s * P:(s + 1) * P],
                                  gu_hi[:, s].bitcast(f32), ALU.subtract).then_inc(gu_lo_done, 1)

            def split_d(c):
                if not c.exists():
                    return
                s, pair = c.c % 2, c.c // 2 % 2
                after(dve, d_hi_done, c.count(1, 1))
                dve.tensor_tensor(d_lo[:, s], raw_d[:, pair, s, :], d_hi[:, s].bitcast(f32),
                                  ALU.subtract).then_inc(d_lo_done, 1)

            thr_f = thr[:].bitcast(f32)
            dve.tensor_scalar(gt[:], key[:], thr_f, 0.0, ALU.is_gt, ALU.add, accum_out=cgt[:]).then_inc(tallied, 1)
            link(dve.tensor_scalar(eq[:], key[:], thr_f, None, ALU.is_equal))
            dve.scalar_tensor_tensor(eqv[:], key[:], 0.0, eq[:], ALU.is_gt, ALU.mult,
                                     accum_out=ceq[:]).then_inc(tallied, 1)
            dve.wait_ge(tallied, 2)
            split_d(Chunk(0, 0, 0))
            dve.wait_ge(tally_sum, 1)
            link(dve.tensor_scalar(ned[:], gb[:, 0:1], -1.0, float(CAP), ALU.mult, ALU.add))
            link(dve.tensor_copy(off[:], gb[:, 1:2]))
            link(dve.tensor_tensor_scan(scan[:], eqv[:], zrow[:], off[:], ALU.add, ALU.add))
            link(dve.tensor_tensor(scan[:], scan[:], eqv[:], ALU.subtract))
            link(dve.scalar_tensor_tensor(eqv[:], scan[:], ned[:], eqv[:], ALU.is_lt, ALU.mult))
            dve.scalar_tensor_tensor(keep[:], gt[:], 1.0, eqv[:], ALU.mult, ALU.add,
                                     accum_out=ckp[:]).then_inc(kept, 1)
            dve.wait_ge(kept, 1)
            split_gu(Chunk(0, 0, 0))
            dve.wait_ge(kept_sum, 1)
            link(dve.tensor_copy(off[:], gb[:, 0:1]))
            link(dve.tensor_tensor_scan(scan[:], keep[:], zrow[:], off[:], ALU.add, ALU.add))
            link(dve.tensor_tensor(scan[:], scan[:], keep[:], ALU.mult))
            dve.tensor_scalar(posm[:], scan[:], -1.0, None, ALU.add).then_inc(posm_done, 1)
            split_gu(Chunk(0, 0, 1))
            dve.wait_ge(pos_turned, 1)
            link(dve.tensor_copy(pos[:].rearrange("p two e s -> p (two e s)"), ub[:, 0:2 * P]))
            posv = pos[:].rearrange("p two e s -> p e s two")
            link(dve.tensor_copy(posi[:], posv))
            dve.tensor_scalar(hi_[:], posi[:], TILE_BITS, None, ALU.arith_shift_right).then_inc(slots_done, 1)
            dve.tensor_scalar(lo_[:], posi[:], P - 1, None, ALU.bitwise_and).then_inc(slots_done, 1)
            dve.wait_ge(slots_done, 2)
            dve.wait_ge(values_done, 1)
            make_values(dve, 0)
            for piece in range(4):
                make_hots(dve, 0, piece)

            def read_list(e):
                after(dve, list_product, e + 1)
                dve.tensor_copy(lst[:].rearrange("p c v -> p (c v)"), ga[:, 0:CT * NV]).then_inc(list_read, 1)
                after(dve, list_read, e + 1)
                dve.scalar_tensor_tensor(lid[:], lst[:, :, 0], float(P), lst[:, :, 1], ALU.mult,
                                         ALU.add).then_inc(list_step, 1)
                dve.tensor_tensor(lw[:], lst[:, :, 5], lst[:, :, 4], ALU.add).then_inc(list_step, 1)
                after(dve, list_step, e * 3 + 2)
                dve.scalar_tensor_tensor(lid2[:], lst[:, :, 2], -8192.0, lid[:], ALU.mult,
                                         ALU.add).then_inc(list_step, 1)
                after(dve, list_step, e * 3 + 3)
                dve.tensor_scalar(sidx_next[:], lid2[:], 8192.0, None, ALU.add)\
                   .then_inc(slots_listed, 1)
                dve.tensor_tensor(wslot_next[:], lw[:], lst[:, :, 3], ALU.add).then_inc(slots_listed, 1)
                for t in range(CT):
                    after(dve, gathered[t], e * 16)
                dve.tensor_copy(gidx[:], lid[:]).then_inc(list_made, 1)

            def move_slots(e):
                after(dve, slots_listed, e * 2 + 2)
                after(dve, scattered, e * (16 * CT))
                after(dve, ys_act, e * 3)
                dve.tensor_copy(sidx[:], sidx_next[:]).then_inc(slots_moved, 1)
                dve.tensor_copy(wslot[:], wslot_next[:]).then_inc(slots_moved, 1)
                after(dve, slots_moved, e * 2 + 2)

            def turned(e, tiles):
                for t in tiles:
                    after(dve, xT_hi_done, e * CT + (t + 1))
                    part = slice(t * P, (t + 1) * P)
                    dve.tensor_tensor(xT_lo[:, :, part],
                                      [ga, gb, ub][t % 3][:].rearrange("p (k n) -> p k n", k=KC),
                                      xT_hi[:, :, part].bitcast(f32), ALU.subtract).then_inc(xT_lo_done, 1)

            read_list(0)
            turned(0, range(CT))

            def expert(e, more):
                def chunk(c):
                    s = c.c % 2
                    if c.c == FC - 2:
                        move_slots(e)
                    after(dve, sil_done, c.count(2, 1))
                    after(dve, h_lo_done, c.count(1, 0))
                    dve.tensor_tensor(hid[:, 0:NA], sil[:, 0:NA], ga[:, NA:2 * NA], ALU.mult).then_inc(hid_done, 1)
                    after(dve, sil_done, c.count(2, 2))
                    after(dve, ub_product, c.count(1, 1))
                    dve.tensor_tensor(hid[:, NA:CAP], sil[:, NA:CAP], ub[:, 0:NB], ALU.mult).then_inc(hid_done, 1)
                    if c.c == FC - 1 and more:
                        turned(e + 1, range(1))
                    split_gu(c.ahead(2))
                    after(dve, h_hi_done, c.count(1, 1))
                    dve.tensor_tensor(h_lo[:, s, :], hid[:], h_hi[:, s, :].bitcast(f32),
                                      ALU.subtract).then_inc(h_lo_done, 1)
                    if c.c == FC - 2 and more:
                        read_list(e + 1)
                    split_d(c.ahead(1))
                    if c.c == 0 and more:
                        make_values(dve, e + 1)
                    if c.c == 1 and more:
                        make_hots(dve, e + 1, 0)
                    if c.c == 4 and more:
                        make_hots(dve, e + 1, c.k + 1)

                run_chunks(dve, e, chunk)
                if more:
                    turned(e + 1, range(1, CT))
                after(dve, scattered, e * (16 * CT))
                for t in range(3, CT):
                    if t < CT - 1:
                        after(dve, y_finished, e * (CT - 1) + (t + 1))
                    else:
                        after(dve, y_product, e * FC + FC)
                    dve.tensor_scalar(ys[:, t, :], y[t][:], wslot[:, t:t + 1], None, ALU.mult).then_inc(ys_dve, 1)

            run_experts(dve, expert)

        @block.tensor
        def _(pe):
            pe.wait_ge(consts, 15)
            pe.wait_ge(wt_done, 1)
            for two in range(2):
                last = pe.transpose(ga[:, two * P:(two + 1) * P], wt[:, two].rearrange("p e s -> p (e s)"), ident[:])
            last.then_inc(wt_turned, 1)
            for u in range(HIGH):
                pe.wait_ge(counted, 3 * u + 3)
                pe.matmul(gb[:, 0:3], same_b[:], cnt3[:], start=True, stop=True).then_inc(totalled, 1)
            with pe.Fori(0, (PAIRS_OF_BITS - HIGH) // SEARCH) as turn:
                for u in range(SEARCH):
                    pe.wait_ge(counted, turn * (3 * SEARCH) + (3 * HIGH + 3 * u + 3))
                    pe.matmul(gb[:, 0:3], same_b[:], cnt3[:], start=True, stop=True).then_inc(totalled, 1)
            pe.wait_ge(tallied, 2)
            pe.wait_ge(thr_done, PAIRS_OF_BITS)
            pe.matmul(gb[:, 0:1], same[:], cgt[:], start=True, stop=True)
            pe.matmul(gb[:, 1:2], before[:], ceq[:], start=True, stop=True).then_inc(tally_sum, 1)
            pe.wait_ge(kept, 1)
            pe.matmul(gb[:, 0:1], before[:], ckp[:], start=True, stop=True).then_inc(kept_sum, 1)
            pe.wait_ge(posm_done, 1)
            for two in range(2):
                last = pe.transpose(ub[:, two * P:(two + 1) * P], posm[:, two * P:(two + 1) * P], ident[:])
            last.then_inc(pos_turned, 1)

            def make_list(e):
                after(pe, vhot_done, e + 1)
                for t in range(T32):
                    if t % HOT == 0:
                        after(pe, hot_done, e * 4 + (t // HOT + 1))
                    last = pe.matmul(ga[:, 0:CT * NV], hot[:, t, :], vhot[:, t].rearrange("p c v -> p (c v)"),
                                     start=(t == 0), stop=(t == T32 - 1))
                last.then_inc(list_product, 1)

            def turn(e, t):
                after(pe, gathered[t], e * 16 + 16)
                if t >= 3:
                    after(pe, xT_lo_done, e * CT + (t - 2))
                for k in range(KC):
                    last = pe.transpose([ga, gb, ub][t % 3][:, k * P:(k + 1) * P],
                                        xg[:, t, k * P:(k + 1) * P], ident[:])
                last.then_inc(xg_turned, 1)

            make_list(0)
            pe.wait_ge(list_read, 1)
            for t in range(CT):
                turn(0, t)

            def up(c):
                s = c.c % 2
                w_, x_ = (gu_hi, gu_lo), (xT_hi, xT_lo)
                for bank_, cols, which, t0, n_, sem_ in (
                        (ga, 0, 0, 0, NA, None), (ga, NA, 1, 0, NA, a_product),
                        (gb, 0, 0, NA, NB, gb_product), (ub, 0, 1, NA, NB, ub_product)):
                    for i, (a, b) in enumerate(PARTS):
                        for k in range(KC):
                            last = pe.matmul(bank_[:, cols:cols + n_], w_[a][:, s, which, k, :],
                                             x_[b][:, k, t0:t0 + n_],
                                             start=(i == 0 and k == 0), stop=(i == 2 and k == KC - 1))
                    if sem_ is not None:
                        last.then_inc(sem_, 1)
                    if c.c == 0 and sem_ is a_product:
                        after(pe, xT_lo_done, c.e * CT + CT)

            def down(c, start, stop):
                s = c.c % 2
                after(pe, h_lo_done, c.count(1, 1))
                after(pe, d_lo_done, c.count(1, 1))
                h_, d_ = (h_hi, h_lo), (d_hi, d_lo)
                for t in range(CT):
                    for i, (a, b) in enumerate(PARTS):
                        last = pe.matmul(y[t][:], h_[a][:, s, t * P:(t + 1) * P], d_[b][:, s, :],
                                         start=(start and i == 0), stop=(stop and i == 2))
                    if stop and t < CT - 1:
                        last.then_inc(y_finished, 1)
                last.then_inc(y_product, 1)

            def expert(e, more):
                def chunk(c):
                    after(pe, gu_lo_done, c.count(1, 1))
                    if c.c == 0:
                        after(pe, xT_lo_done, e * CT + 4)
                    else:
                        after(pe, hid_done, c.count(2, 0))
                    if c.c == FC - 1 and more:
                        after(pe, list_read, e + 2)
                    up(c)
                    if c.c == FC - 2 and more:
                        after(pe, hid_done, c.count(2, 1))
                        make_list(e + 1)
                    if c.c == FC - 1 and more:
                        after(pe, hid_done, c.count(2, 1))
                        turn(e + 1, 0)
                    if c.c == 1:
                        after(pe, ys_act, e * 3)
                        after(pe, ys_dve, e * 2)
                    if c.c > 0:
                        down(c.ahead(-1), start=(c.c == 1), stop=False)

                run_chunks(pe, e, chunk)
                last_chunk = Chunk(e, 0, FC - 1)
                if more:
                    after(pe, hid_done, last_chunk.count(2, 2))
                    for t in range(1, 4):
                        turn(e + 1, t)
                down(last_chunk, start=False, stop=True)
                if more:
                    turn(e + 1, 4)

            run_experts(pe, expert)


def build(nc, x, context, energy, Wq, bq, Wk, bk, Wv, bv, Wo, bo, router_w, wg, wu, wd, out):
    xn2 = nc.dram_tensor("xn2", [N, D], f32, kind="Internal").ap()
    vblocks = nc.dram_tensor("vblocks", [B, KC, GS, P], f32, kind="Internal").ap()
    with nc.sbuf_tensor("logits", [P, B, TILES // B, E], f32) as logits:
        with ExitStack() as ctx:
            attention(nc, ctx, x, context, energy, Wq, bq, Wk, bk, Wv, bv, Wo, bo, router_w, out,
                      xn2, vblocks, logits)
        with ExitStack() as ctx:
            experts(nc, ctx, logits, wg, wu, wd, out, xn2)


_INS = ["x", "ctx_1024", "ctxb_2048x32", "L0_xattn_Wq", "L0_xattn_bq", "L0_xattn_Wk", "L0_xattn_bk",
        "L0_xattn_Wv", "L0_xattn_bv", "L0_xattn_Wo", "L0_xattn_bo", "L0_ffn_router_w", "L0_ffn_wg",
        "L0_ffn_wu", "L0_ffn_wd"]
_OUTS = [((B, L, D), "float32")]


def kernel(**inputs):
    import numpy as _np
    import concourse.bacc as _bacc
    from concourse import mybir as _mybir
    from concourse.bass_utils import run_bass_kernel_spmd as _run

    nc = _bacc.Bacc("TRN2", target_bir_lowering=False, num_devices=1)
    arrays, args = {}, []
    for name in _INS:
        a = _np.ascontiguousarray(inputs[name])
        arrays[f"in_{name}_dram"] = a
        args.append(nc.dram_tensor(f"in_{name}_dram", a.shape, _mybir.dt.from_np(a.dtype), kind="ExternalInput").ap())
    for i, (shape, dtype) in enumerate(_OUTS):
        dt = _mybir.dt.from_np(_np.dtype(dtype))
        args.append(nc.dram_tensor(f"out_{i}_dram", shape, dt, kind="ExternalOutput").ap())
    build(nc, *args)
    r = _run(nc, [arrays], core_ids=[0])
    got = tuple(r.results[0][f"out_{i}_dram"] for i in range(len(_OUTS)))
    return got[0]
```
